# Optimizing a Trainium2 kernel written in Bass

```python
import numpy as np
import jax
import jax.numpy as jnp

def _softmax(x, axis=-1):
    return jax.nn.softmax(x, axis=axis)

def _gelu(x):
    return jax.nn.gelu(x, approximate=True)

def _silu(x):
    return jax.nn.silu(x)

def _sigmoid(x):
    return jax.nn.sigmoid(x)

def _layernorm(x, axis=-1, eps=1e-05):
    m = jnp.mean(x, axis=axis, keepdims=True)
    v = jnp.var(x, axis=axis, keepdims=True)
    return (x - m) / jnp.sqrt(v + eps)

def _scatter_add(tgt, idx, src, axis=0):
    return tgt.at[idx].add(src)

def _segment_sum(src, seg, n):
    return jax.ops.segment_sum(src, seg, n)
kernel_name = 'mk_sandwich_d1_jaxref_r4_2f2175'

def setup_inputs(seed: int=0):
    np.random.seed(seed)
    _w = jnp.asarray

    def _L0_attn_setup():
        import jax, jax.numpy as jnp
        import numpy as np
        B, T, C = (1, 1024, 512)
        H = 16
        D = C // H
        BLOCK = 64
        WINDOW = 256
        DILATION = 64
        GLOBAL_TOKENS = 128
        ROPE_BASE = 10000.0
        SCALE = 1.0 / np.sqrt(D)

        def _rope(x):
            t = jnp.arange(x.shape[2], dtype=jnp.float32)
            inv_freq = 1.0 / ROPE_BASE ** (jnp.arange(0, D, 2, dtype=jnp.float32) / D)
            freqs = jnp.outer(t, inv_freq)
            emb = jnp.concatenate([freqs, freqs], axis=-1)
            cos = jnp.cos(emb)[None, None].astype(x.dtype)
            sin = jnp.sin(emb)[None, None].astype(x.dtype)
            x1, x2 = jnp.split(x, 2, axis=-1)
            rot = jnp.concatenate([-x2, x1], axis=-1)
            return x * cos + rot * sin

        def _token_mask(seq_len):
            nb = (seq_len + BLOCK - 1) // BLOCK
            bp = jnp.arange(nb)
            qb, kb = (bp[:, None], bp[None, :])
            dist = qb - kb
            window_blocks = WINDOW // BLOCK
            window_mask = (dist >= 0) & (dist <= window_blocks)
            global_blocks = max(1, GLOBAL_TOKENS // BLOCK)
            global_mask = kb < global_blocks
            dilation_blocks = max(1, DILATION // BLOCK)
            dilated_mask = kb % dilation_blocks == 0
            causal_mask = kb <= qb
            block_mask = (window_mask | global_mask | dilated_mask) & causal_mask
            tok = jnp.repeat(jnp.repeat(block_mask, BLOCK, axis=0), BLOCK, axis=1)
            return tok[:seq_len, :seq_len]
        key = jax.random.key(seed)
        ks = jax.random.split(key, 5)
        x = jax.random.normal(ks[0], (B, T, C), dtype=jnp.float32)
        w_q = jax.random.normal(ks[1], (C, C), dtype=jnp.float32) * 0.02
        w_k = jax.random.normal(ks[2], (C, C), dtype=jnp.float32) * 0.02
        w_v = jax.random.normal(ks[3], (C, C), dtype=jnp.float32) * 0.02
        w_o = jax.random.normal(ks[4], (C, C), dtype=jnp.float32) * 0.02
        return {'x': x, 'w_q': w_q, 'w_k': w_k, 'w_v': w_v, 'w_o': w_o}
    _L0_attn_in = _L0_attn_setup()

    def _L0_ffn_setup():
        import jax, jax.numpy as jnp
        import numpy as np
        E, R, K = (8, 8, 2)
        D, F = (512, 2048)
        B, S = (2, 512)
        SCALING = 16.0 / 8.0

        def act(x):
            return jax.nn.gelu(x, approximate=True)
        key = jax.random.key(seed)
        ks = jax.random.split(key, 12)
        return {'hidden_states': jax.random.normal(ks[0], (B, S, D), jnp.float32), 'W_r': jax.random.normal(ks[1], (E, D), jnp.float32) * 0.02, 'b_r': jnp.zeros((E,), jnp.float32), 'W1': jax.random.normal(ks[2], (F, D), jnp.float32) * 0.02, 'b1': jnp.zeros((F,), jnp.float32), 'W2': jax.random.normal(ks[3], (D, F), jnp.float32) * 0.02, 'b2': jnp.zeros((D,), jnp.float32), 'A1': jax.random.normal(ks[4], (E, R, D), jnp.float32) * 0.02, 'B1': jax.random.normal(ks[5], (F, R) * 1 + ()).reshape(1, F, R).repeat(1, 0) * 0.0 + jax.random.normal(ks[5], (E, F, R), jnp.float32) * 0.02, 'A2': jax.random.normal(ks[6], (E, R, F), jnp.float32) * 0.02, 'B2': jax.random.normal(ks[7], (E, D, R), jnp.float32) * 0.02}
    _L0_ffn_in = _L0_ffn_setup()
    _d = {'L0_attn_x': _L0_attn_in['x'], 'L0_attn_w_q': _L0_attn_in['w_q'], 'L0_attn_w_k': _L0_attn_in['w_k'], 'L0_attn_w_v': _L0_attn_in['w_v'], 'L0_attn_w_o': _L0_attn_in['w_o'], 'L0_ffn_W_r': _L0_ffn_in['W_r'], 'L0_ffn_b_r': _L0_ffn_in['b_r'], 'L0_ffn_W1': _L0_ffn_in['W1'], 'L0_ffn_b1': _L0_ffn_in['b1'], 'L0_ffn_W2': _L0_ffn_in['W2'], 'L0_ffn_b2': _L0_ffn_in['b2'], 'L0_ffn_A1': _L0_ffn_in['A1'], 'L0_ffn_B1': _L0_ffn_in['B1'], 'L0_ffn_A2': _L0_ffn_in['A2'], 'L0_ffn_B2': _L0_ffn_in['B2']}
    _x0 = _d['L0_attn_x']
    _d['L0_attn_x'] = jax.random.normal(jax.random.fold_in(jax.random.key(seed), 1), (4, 1024, 512), dtype=_x0.dtype)
    del _x0
    return _d

def reference(L0_attn_x, L0_attn_w_q, L0_attn_w_k, L0_attn_w_v, L0_attn_w_o, L0_ffn_W_r, L0_ffn_b_r, L0_ffn_W1, L0_ffn_b1, L0_ffn_W2, L0_ffn_b2, L0_ffn_A1, L0_ffn_B1, L0_ffn_A2, L0_ffn_B2):

    def _L0_attn_ref(x, w_q, w_k, w_v, w_o):
        import jax, jax.numpy as jnp
        import numpy as np
        B, T, C = (1, 1024, 512)
        H = 16
        D = C // H
        BLOCK = 64
        WINDOW = 256
        DILATION = 64
        GLOBAL_TOKENS = 128
        ROPE_BASE = 10000.0
        SCALE = 1.0 / np.sqrt(D)

        def _rope(x):
            t = jnp.arange(x.shape[2], dtype=jnp.float32)
            inv_freq = 1.0 / ROPE_BASE ** (jnp.arange(0, D, 2, dtype=jnp.float32) / D)
            freqs = jnp.outer(t, inv_freq)
            emb = jnp.concatenate([freqs, freqs], axis=-1)
            cos = jnp.cos(emb)[None, None].astype(x.dtype)
            sin = jnp.sin(emb)[None, None].astype(x.dtype)
            x1, x2 = jnp.split(x, 2, axis=-1)
            rot = jnp.concatenate([-x2, x1], axis=-1)
            return x * cos + rot * sin

        def _token_mask(seq_len):
            nb = (seq_len + BLOCK - 1) // BLOCK
            bp = jnp.arange(nb)
            qb, kb = (bp[:, None], bp[None, :])
            dist = qb - kb
            window_blocks = WINDOW // BLOCK
            window_mask = (dist >= 0) & (dist <= window_blocks)
            global_blocks = max(1, GLOBAL_TOKENS // BLOCK)
            global_mask = kb < global_blocks
            dilation_blocks = max(1, DILATION // BLOCK)
            dilated_mask = kb % dilation_blocks == 0
            causal_mask = kb <= qb
            block_mask = (window_mask | global_mask | dilated_mask) & causal_mask
            tok = jnp.repeat(jnp.repeat(block_mask, BLOCK, axis=0), BLOCK, axis=1)
            return tok[:seq_len, :seq_len]
        Bc, Tc, Cc = x.shape
        q = (x @ w_q.T).reshape(Bc, Tc, H, D).transpose(0, 2, 1, 3)
        k = (x @ w_k.T).reshape(Bc, Tc, H, D).transpose(0, 2, 1, 3)
        v = (x @ w_v.T).reshape(Bc, Tc, H, D).transpose(0, 2, 1, 3)
        q = _rope(q)
        k = _rope(k)
        scores = jnp.einsum('bhqd,bhkd->bhqk', q, k) * SCALE
        tok_mask = _token_mask(Tc)
        scores = jnp.where(tok_mask[None, None], scores, -jnp.inf)
        attn = jax.nn.softmax(scores, axis=-1)
        ctx = jnp.einsum('bhqk,bhkd->bhqd', attn, v)
        ctx = ctx.transpose(0, 2, 1, 3).reshape(Bc, Tc, Cc)
        return ctx @ w_o.T

    def _L0_ffn_ref(hidden_states, W_r, b_r, W1, b1, W2, b2, A1, B1, A2, B2):
        import jax, jax.numpy as jnp
        import numpy as np
        E, R, K = (8, 8, 2)
        D, F = (512, 2048)
        B, S = (2, 512)
        SCALING = 16.0 / 8.0

        def act(x):
            return jax.nn.gelu(x, approximate=True)
        b, s, d = hidden_states.shape
        N = b * s
        x = hidden_states.reshape(N, d)
        probs = jax.nn.softmax(x @ W_r.T + b_r, axis=-1)
        w_topk, idx_topk = jax.lax.top_k(probs, K)
        base1 = x @ W1.T + b1
        u1 = jnp.einsum('nd,erd->ner', x, A1)
        B1_rf = B1.transpose(0, 2, 1).reshape(E * R, F)
        B2_rf = B2.transpose(0, 2, 1).reshape(E * R, d)
        res = jnp.zeros((N, d), hidden_states.dtype)
        for k in range(K):
            oh = jax.nn.one_hot(idx_topk[:, k], E, dtype=x.dtype)
            z1 = (u1 * oh[:, :, None]).reshape(N, E * R)
            h = act(base1 + z1 @ B1_rf * SCALING)
            u2 = jnp.einsum('nf,erf->ner', h, A2)
            z2 = (u2 * oh[:, :, None]).reshape(N, E * R)
            y = h @ W2.T + b2 + z2 @ B2_rf * SCALING
            res = res + w_topk[:, k:k + 1] * y
        return res.reshape(b, s, d)
    x = L0_attn_x
    x = x + _layernorm(_L0_attn_ref(_layernorm(x, axis=-1), L0_attn_w_q, L0_attn_w_k, L0_attn_w_v, L0_attn_w_o), axis=-1)
    x = x + _layernorm(_L0_ffn_ref(_layernorm(x, axis=-1), L0_ffn_W_r, L0_ffn_b_r, L0_ffn_W1, L0_ffn_b1, L0_ffn_W2, L0_ffn_b2, L0_ffn_A1, L0_ffn_B1, L0_ffn_A2, L0_ffn_B2), axis=-1)
    return x

_drawn_inputs = setup_inputs


def setup_inputs(seed=0):
    import zlib

    import numpy as np

    out = dict(_drawn_inputs(seed))
    spreads = {'L0_ffn_b_r': (0.0, 0.293), 'L0_ffn_b1': (0.0, 0.1), 'L0_ffn_b2': (0.0, 0.1)}
    factors = {}
    for name, (base, spread) in spreads.items():
        noise = np.random.default_rng([zlib.crc32(name.encode()), seed]).standard_normal(out[name].shape)
        drawn = base * np.exp(spread * noise) if base else spread * noise
        out[name] = jnp.asarray(drawn.astype(out[name].dtype))
    for name, factor in factors.items():
        out[name] = (out[name] * factor).astype(out[name].dtype)
    return out
```

```python
from contextlib import ExitStack

import numpy as np

import concourse.bass as bass
from concourse import mybir

F32 = mybir.dt.float32
F32R = mybir.dt.float32r
BF16 = mybir.dt.bfloat16
F16 = mybir.dt.float16
ALU = mybir.AluOpType
ACT = mybir.ActivationFunctionType
AX_X = mybir.AxisListType.X

P = 128
EPS = 1e-5

SPLIT_PAIRS = ((0, 0), (1, 0), (0, 1))


class Space:

    def __init__(self, nc, prefix):
        self.nc, self.prefix, self.stack = nc, prefix, ExitStack()

    def __enter__(self):
        return self

    def __exit__(self, *a):
        return self.stack.__exit__(*a)

    def sb(self, name, shape, dt=F32):
        return self.stack.enter_context(self.nc.sbuf_tensor(self.prefix + name, shape, dt))

    def ps(self, name, shape, dt=F32):
        return self.stack.enter_context(self.nc.psum_tensor(self.prefix + name, shape, dt))

    def sem(self, name):
        return self.stack.enter_context(self.nc.semaphore(self.prefix + name))

    def sems(self, name, n):
        return [self.sem(f"{name}{i}") for i in range(n)]

    def block(self):
        return self.stack.enter_context(self.nc.Block())


def wait_apart(eng, sem, value, waited):
    eng.wait_ge(sem, value)
    eng.sem_inc(waited, 1)


def make_norm_constants(nc, pool, norm_consts, made):
    for k, value in enumerate((-0.5, EPS, -1.0)):
        nc.gpsimd.memset(norm_consts[:, k:k + 1], value).then_inc(made, 1)
    pool.wait_ge(made, 3)


def layer_norm_coefficients(nc, pool, norm_consts, mean_var, coef, stats_ready, eps_added, rstd_ready, shift_ready, count):
    neg_half, eps, neg_one = (norm_consts[:, k:k + 1] for k in range(3))
    var_eps, neg_mean, rstd, shift = (coef[:, k:k + 1] for k in range(4))
    pool.wait_ge(stats_ready, count)
    nc.gpsimd.tensor_tensor(var_eps, mean_var[:, 1:2], eps, ALU.add)
    nc.gpsimd.tensor_tensor(neg_mean, mean_var[:, 0:1], neg_one, ALU.mult).then_inc(eps_added, 1)
    pool.wait_ge(eps_added, count)
    nc.gpsimd.tensor_tensor(rstd, var_eps, neg_half, ALU.pow).then_inc(rstd_ready, 1)
    pool.wait_ge(rstd_ready, count)
    nc.gpsimd.tensor_tensor(shift, neg_mean, rstd, ALU.mult).then_inc(shift_ready, 1)


def make_identity(nc, eng, identity, made):
    nc.gpsimd.memset(identity[:], 0.0).then_inc(made, 1)
    eng.wait_ge(made, 1)
    nc.gpsimd.affine_select(out=identity[:], in_=identity[:], compare_op=ALU.not_equal, fill=1.0,
                            base=0, pattern=[[-1, P]], channel_multiplier=1).then_inc(made, 1)


def project_phase(nc, x, w_qkv, rope, q_rows, k_rows, v_rows):
    N, C = x.shape
    T = rope.shape[0]
    NT, CT = N // P, C // P
    TT = T // P
    H, D = C // 32, 32
    with Space(nc, "a_") as s:
        identity = s.sb("identity", [P, P])
        w_raw = s.sb("w_raw", [P, CT, 3 * C])
        w = s.sb("w", [P, 2, CT, 3 * C], F32R)
        rope_sb = s.sb("rope_sb", [P, TT, 2, D])
        x_sb = s.sb("x_sb", [P, 2, C])
        stats = s.sb("stats", [P, 2, 6])
        mean_var = s.sb("mean_var", [P, 2, 2])
        norm_consts = s.sb("norm_consts", [P, 3])
        coef = s.sb("coef", [P, 2, 4])
        xn = s.sb("xn", [P, 2, C])
        xnT = s.sb("xnT", [P, 2, 2, CT, P], F32R)
        by_cos = s.sb("by_cos", [P, 2, 2, C])
        by_sin = s.sb("by_sin", [P, 2, 2, C])
        v_sb = s.sb("v_sb", [P, 2, C])
        ps_xT = s.ps("ps_xT", [P, 2, CT, P])
        ps_qkv = s.ps("ps_qkv", [P, 2, 3, C])

        id_made = s.sem("id_made")
        norm_consts_made = s.sem("norm_consts_made")
        w_loaded = s.sems("w_loaded", CT)
        rope_loaded = s.sem("rope_loaded")
        w_hi_ready, w_lo_ready = s.sem("w_hi_ready"), s.sem("w_lo_ready")
        x_loaded = s.sems("x_loaded", 2)
        bn_ready, stats_ready = s.sem("bn_ready"), s.sem("stats_ready")
        eps_added, rstd_ready, shift_ready = s.sem("eps_added"), s.sem("rstd_ready"), s.sem("shift_ready")
        xn_ready = s.sem("xn_ready")
        xT_in_psum = s.sem("xT_in_psum")
        xT_hi_ready, xT_lo_ready = s.sem("xT_hi_ready"), s.sem("xT_lo_ready")
        projected = s.sem("projected")
        rope_parts = s.sem("rope_parts")
        rotated = s.sem("rotated")
        v_ready = s.sem("v_ready")
        qk_free, v_free = s.sems("qk_free", 2), s.sems("v_free", 2)
        waited = s.sem("waited")
        block = s.block()

        @block.sync
        def _(sp):
            wr = w_qkv.rearrange("(c p) o -> p c o", p=P)

            def load(m, u):
                sp.dma_start(x_sb[:, u], x[bass.ds(m * P, P), :]).then_inc(x_loaded[u], 16)

            load(0, 0)
            load(1, 1)
            for c in range(CT):
                sp.dma_start(w_raw[:, c], wr[:, c]).then_inc(w_loaded[c], 16)
            sp.dma_start(rope_sb[:], rope.rearrange("(t p) r -> p t r", p=P)
                         .rearrange("p t (a d) -> p t a d", a=2)).then_inc(rope_loaded, 16)
            for u in range(2):
                sp.sem_inc(qk_free[u], 32)
                sp.sem_inc(v_free[u], 16)

            def tile(n, u, it, last):
                if not last:
                    sp.wait_ge(xn_ready, n + 1)
                    load(n + 2, u)
                sp.wait_ge(rotated, 2 * n + 1)
                sp.dma_start(q_rows[bass.ds(n * P, P), :], by_cos[:, u, 0]).then_inc(qk_free[u], 16)
                sp.wait_ge(rotated, 2 * n + 2)
                sp.dma_start(k_rows[bass.ds(n * P, P), :], by_cos[:, u, 1]).then_inc(qk_free[u], 16)
                sp.wait_ge(v_ready, n + 1)
                sp.dma_start(v_rows[bass.ds(n * P, P), :], v_sb[:, u]).then_inc(v_free[u], 16)

            with sp.Fori(0, NT // 2 - 1) as it:
                for u in range(2):
                    tile(2 * it + u, u, it, False)
            for u in range(2):
                tile(NT - 2 + u, u, NT // 2 - 1, True)
            for u in range(2):
                sp.wait_ge(qk_free[u], 32 * (NT // 2 + 1))
                sp.wait_ge(v_free[u], 16 * (NT // 2 + 1))

        @block.gpsimd
        def _(pool):
            make_identity(nc, pool, identity, id_made)
            make_norm_constants(nc, pool, norm_consts, norm_consts_made)

            def coefficients(m, u):
                layer_norm_coefficients(nc, pool, norm_consts, mean_var[:, u], coef[:, u],
                                        stats_ready, eps_added, rstd_ready, shift_ready, m + 1)

            coefficients(0, 0)
            coefficients(1, 1)

            def tile(n, u, last):
                if not last:
                    coefficients(n + 2, u)
                for j in range(2):
                    pool.wait_ge(rope_parts, 2 * n + j + 1)
                    nc.gpsimd.tensor_tensor(by_cos[:, u, j], by_cos[:, u, j], by_sin[:, u, j], ALU.add).then_inc(rotated, 1)

            with pool.Fori(0, NT // 2 - 1) as it:
                for u in range(2):
                    tile(2 * it + u, u, False)
            for u in range(2):
                tile(NT - 2 + u, u, True)

        @block.scalar
        def _(act):
            def normalise(m, u):
                act.wait_ge(shift_ready, m + 1)
                nc.scalar.activation(xn[:, u], x_sb[:, u], ACT.Identity, bias=coef[:, u, 3:4],
                                     scale=coef[:, u, 2:3]).then_inc(xn_ready, 1)

            def take_hi(m, u, it):
                act.wait_ge(xT_in_psum, m + 1)
                if it is not None:
                    act.wait_ge(projected, 3 * m - 3)
                nc.scalar.activation(xnT[:, u, 0], ps_xT[:, u], ACT.Copy).then_inc(xT_hi_ready, 1)

            normalise(0, 0)
            for c in range(CT):
                act.wait_ge(w_loaded[c], 16)
                nc.scalar.activation(w[:, 0, c], w_raw[:, c], ACT.Copy).then_inc(w_hi_ready, 1)
            take_hi(0, 0, None)
            normalise(1, 1)

            def tile(n, u, it, last):
                if not (last and u == 1):
                    if isinstance(n, int) and n == 0:
                        take_hi(1, 1, None)
                    else:
                        take_hi(n + 1, 1 - u, it)
                if not last:
                    normalise(n + 2, u)
                act.wait_ge(projected, 3 * n + 3)
                act.wait_ge(v_free[u], 16 * (it + 1))
                nc.scalar.activation(v_sb[:, u], ps_qkv[:, u, 2], ACT.Copy).then_inc(v_ready, 1)

            for u in range(2):
                tile(u, u, 0, False)
            with act.Fori(1, NT // 2 - 1) as it:
                for u in range(2):
                    tile(2 * it + u, u, it, False)
            for u in range(2):
                tile(NT - 2 + u, u, NT // 2 - 1, True)

        @block.vector
        def _(dve):
            def statistics(m, u, it):
                dve.wait_ge(x_loaded[u], 16 * (it + 1))
                nc.vector.bn_stats(stats[:, u], x_sb[:, u]).then_inc(bn_ready, 1)
                wait_apart(dve, bn_ready, m + 1, waited)
                nc.vector.bn_aggr(mean_var[:, u], stats[:, u]).then_inc(stats_ready, 1)

            def take_lo(m, u):
                dve.wait_ge(xT_hi_ready, m + 1)
                nc.vector.tensor_tensor(xnT[:, u, 1], ps_xT[:, u], xnT[:, u, 0].bitcast(F32), ALU.subtract).then_inc(xT_lo_ready, 1)

            statistics(0, 0, 0)
            statistics(1, 1, 0)
            for c in range(CT):
                dve.wait_ge(w_hi_ready, c + 1)
                nc.vector.tensor_tensor(w[:, 1, c], w_raw[:, c], w[:, 0, c].bitcast(F32), ALU.subtract).then_inc(w_lo_ready, 1)
            take_lo(0, 0)
            dve.wait_ge(rope_loaded, 16)

            def rope_tile(n, u, it, t):
                cos = rope_sb[:, t, 0].unsqueeze(1).broadcast_to([P, H, D])
                for j in range(2):
                    src = ps_qkv[:, u, j].rearrange("p (h d) -> p h d", d=D)
                    dve.wait_ge(projected, 3 * n + j + 1)
                    dve.wait_ge(qk_free[u], 32 * (it + 1))
                    nc.vector.tensor_tensor(by_cos[:, u, j].rearrange("p (h d) -> p h d", d=D), src, cos, ALU.mult)
                    dst = by_sin[:, u, j].rearrange("p (h d) -> p h d", d=D)
                    half = D // 2
                    for a, b in ((0, half), (half, 0)):
                        sin = rope_sb[:, t, 1, a:a + half].unsqueeze(1).broadcast_to([P, H, half])
                        last = nc.vector.tensor_tensor(dst[:, :, a:a + half], src[:, :, b:b + half], sin, ALU.mult)
                    last.then_inc(rope_parts, 1)

            def tile(n, u, it, t, last):
                if not (last and u == 1):
                    take_lo(n + 1, 1 - u)
                if not last:
                    statistics(n + 2, u, it + 1)
                rope_tile(n, u, it, t)

            reps = NT // TT
            with dve.Fori(0, reps - 1) as b:
                for t in range(TT):
                    tile(b * TT + t, t % 2, b * (TT // 2) + t // 2, t, False)
            for t in range(TT):
                n = (reps - 1) * TT + t
                tile(n, t % 2, n // 2, t, t >= TT - 2)

        @block.tensor
        def _(pe):
            def transpose(m, u, it):
                pe.wait_ge(xn_ready, m + 1)
                if it is not None:
                    pe.wait_ge(xT_lo_ready, m - 1)
                for c in range(CT):
                    last = nc.tensor.transpose(ps_xT[:, u, c], xn[:, u, c * P:(c + 1) * P], identity[:])
                last.then_inc(xT_in_psum, 1)

            pe.wait_ge(id_made, 2)
            transpose(0, 0, None)
            pe.wait_ge(w_lo_ready, CT)

            def project(n, u, it):
                pe.wait_ge(xT_lo_ready, n + 1)
                for j in range(3):
                    if it is not None:
                        if j < 2:
                            pe.wait_ge(rope_parts, 2 * n - 3 + j)
                        else:
                            pe.wait_ge(v_ready, n - 1)
                    k = 0
                    for c in range(CT):
                        for a, b in SPLIT_PAIRS:
                            last = nc.tensor.matmul(ps_qkv[:, u, j], xnT[:, u, a, c], w[:, b, c, j * C:(j + 1) * C],
                                                    start=k == 0, stop=k == 3 * CT - 1)
                            k += 1
                    last.then_inc(projected, 1)

            for n in range(2):
                transpose(n + 1, 1 - n, None if n == 0 else 0)
                project(n, n, None)
            with pe.Fori(1, NT // 2 - 1) as it:
                for u in range(2):
                    transpose(2 * it + u + 1, 1 - u, it)
                    project(2 * it + u, u, it)
            transpose(NT - 1, 1, 0)
            project(NT - 2, 0, 0)
            project(NT - 1, 1, 0)


def attention_phase(nc, q_rows, k_rows, v_rows, aux_q, aux_k, q_first_of_block, ctx_rows):
    N, C = q_rows.shape
    T = aux_q.shape[1]
    B = N // T
    HI = 4
    HG = C // (HI * 32)
    ITEMS = B * HG
    D = 32
    W = HI * D
    TT = T // P
    G = 512
    GT = G // P
    NG = T // G
    AUX = 96
    MROW = AUX + 16
    VW = 1 + 3 * D
    SCALE = 1.0 / float(np.sqrt(D))

    first = []
    for t in range(TT):
        n = (t + 1) * P
        for part in range((n + G - 1) // G):
            first.append((t, part * G, min(G, n - part * G), part))
    second = [(g, kt, max(0, kt - GT * g)) for g in range(NG) for kt in range(GT * (g + 1))]
    NF, NS = len(first), len(second)
    assert NF == NS == 12 and NG == 2
    FG0 = sum(1 for f in first if f[0] < GT)
    POOL_LO = (2, 3, 6, 9, 11)
    DVE_LO = tuple(j for j in range(NS) if j not in POOL_LO)
    MISC = (("shift1", 0), ("stack", 2), ("stack", 4), ("stack", 6), ("stack", 8), ("shift0", 9))
    NM = len(MISC)
    LAG = 2
    RP = 3
    PV0, SF0, CF0 = RP, 2, NG

    with Space(nc, "b_") as s:
        identity = s.sb("identity", [P, P])
        identity_r = s.sb("identity_r", [P, P], F32R)
        aux_raw = s.sb("aux_raw", [32, 2, T])
        qf_raw = s.sb("qf_raw", [P, TT, 16])
        q_in = s.sb("q_in", [P, 2, TT, W])
        k_in = s.sb("k_in", [P, 2, TT, W])
        v_in = s.sb("v_in", [P, 2, TT, W])
        q96 = s.sb("q96", [P, 2, TT, HI, 3 * D], F32R)
        k96 = s.sb("k96", [P, 2, TT, HI, 3 * D], F32R)
        v_rest = s.sb("v_rest", [P, 2, TT, W])
        v3 = s.sb("v3", [P, 2, TT, HI, VW], BF16)
        qT = s.sb("qT", [P, 2, HI, T], F32R)
        kT = s.sb("kT", [P, 2, HI, T], F32R)
        shiftc = s.sb("shiftc", [P, TT, P], F32R)
        pmax = s.sb("pmax", [P, TT, 2])
        negmax = s.sb("negmax", [P, TT])
        prob = s.sb("prob", [P, RP, G])
        p_hi = s.sb("p_hi", [P, RP, G], F16)
        p_lo = s.sb("p_lo", [P, RP, G], F16)
        parts = s.sb("parts", [P, 2, GT, D])
        recip = s.sb("recip", [P, 2, GT])
        ctx_sb = s.sb("ctx_sb", [P, 2, TT, W])
        ps_first = s.ps("ps_first", [P, 2, G])
        ps_second = s.ps("ps_second", [P, 2, G])
        ps_misc = s.ps("ps_misc", [P, 2, G])
        ps_ctx = s.ps("ps_ctx", [P, 2, G])

        id_made, id_r_made = s.sem("id_made"), s.sem("id_r_made")
        aux_loaded = s.sem("aux_loaded")
        zeroed, aux_ready, shiftc_ready, ones_made = (s.sem(x) for x in ("zeroed", "aux_ready", "shiftc_ready", "ones_made"))
        q_loaded, k_loaded, v_loaded = s.sems("q_loaded", 2), s.sems("k_loaded", 2), s.sems("v_loaded", 2)
        hi_made, qk_split = s.sem("hi_made"), s.sem("qk_split")
        v_stage, v_split = s.sem("v_stage"), s.sem("v_split")
        first_done, first_read = s.sem("first_done"), s.sem("first_read")
        negmax_made, shift_hi_made, shift_written = s.sem("negmax_made"), s.sem("shift_hi_made"), s.sem("shift_written")
        misc_full, misc_free = s.sem("misc_full"), s.sem("misc_free")
        second_done = s.sem("second_done")
        prob_ready, p_hi_ready = s.sem("prob_ready"), s.sem("p_hi_ready")
        lo_dve, lo_pool = s.sem("lo_dve"), s.sem("lo_pool")
        pv_done = s.sem("pv_done")
        parts_ready, ctx_ready = s.sem("parts_ready"), s.sem("ctx_ready")
        ctx_stored = s.sems("ctx_stored", 2)
        waited = s.sem("waited")
        block = s.block()

        def pairs(eng, step):
            with eng.Fori(0, ITEMS // 2 - 1) as it:
                for u in range(2):
                    for h in range(HI):
                        step(2 * it + u, u, h, it, False)
            for u in range(2):
                for h in range(HI):
                    step(ITEMS - 2 + u, u, h, ITEMS // 2 - 1, True)

        def splits_item(u, last):
            return not last

        def stacks_item(u, last):
            return not (last and u == 1)

        def has_next_step(u, h, last):
            return not (last and u == 1 and h == HI - 1)

        def step_of(i, h):
            return HI * i + h

        @block.sync
        def _(sp):
            sp.dma_start(aux_raw[:, 0], aux_q).then_inc(aux_loaded, 16)
            sp.dma_start(aux_raw[:, 1], aux_k).then_inc(aux_loaded, 16)
            sp.dma_start(qf_raw[:], q_first_of_block.rearrange("(t p) b -> p t b", p=P)).then_inc(aux_loaded, 16)

            def load(i, u):
                row, col = (i // HG) * T, (i % HG) * W
                for dst, src, sem in ((q_in, q_rows, q_loaded), (k_in, k_rows, k_loaded), (v_in, v_rows, v_loaded)):
                    sp.dma_start(dst[:, u], src[bass.ds(row, T), bass.ds(col, W)].rearrange("(t p) w -> p t w", p=P)).then_inc(sem[u], 16)

            load(0, 0)
            load(1, 1)
            for u in range(2):
                sp.sem_inc(ctx_stored[u], 16)
            sp.wait_ge(qk_split, HI)
            sp.wait_ge(v_split, 1)
            load(2, 0)
            sp.wait_ge(qk_split, 2 * HI)
            sp.wait_ge(v_split, 2)
            load(3, 1)

            def store(i, u):
                row, col = (i // HG) * T, (i % HG) * W
                sp.dma_start(ctx_rows[bass.ds(row, T), bass.ds(col, W)].rearrange("(t p) w -> p t w", p=P), ctx_sb[:, u]).then_inc(ctx_stored[u], 16)

            with sp.Fori(0, ITEMS // 2 - 2) as it:
                for u in range(2):
                    sp.wait_ge(ctx_ready, CF0 + NG * HI * (2 * it + u + 1))
                    store(2 * it + u, u)
                    sp.wait_ge(qk_split, HI * (2 * it + u + 3))
                    sp.wait_ge(v_split, 2 * it + u + 3)
                    load(2 * it + u + 4, u)
            for i in range(ITEMS - 4, ITEMS):
                sp.wait_ge(ctx_ready, CF0 + NG * HI * (i + 1))
                store(i, i % 2)
            for u in range(2):
                sp.wait_ge(ctx_stored[u], 16 * (ITEMS // 2 + 1))

        @block.gpsimd
        def _(pool):
            make_identity(nc, pool, identity, id_made)
            nc.gpsimd.memset(v3[:, :, :, :, 0:1], 1.0).then_inc(ones_made, 1)
            def split_v(i, u):
                stage = 4 * i
                vin = v_in[:, u].rearrange("p t (h d) -> p (t h) d", d=D)
                rest = v_rest[:, u].rearrange("p t (h d) -> p (t h) d", d=D)
                rows = v3[:, u].rearrange("p t h w -> p (t h) w")
                part = [rows[:, :, 1 + D * k:1 + D * (k + 1)] for k in range(3)]
                nc.gpsimd.tensor_copy(part[0], vin).then_inc(v_stage, 1)
                wait_apart(pool, v_stage, stage + 1, waited)
                nc.gpsimd.tensor_tensor(rest, vin, part[0], ALU.subtract).then_inc(v_stage, 1)
                wait_apart(pool, v_stage, stage + 2, waited)
                nc.gpsimd.tensor_copy(part[1], rest).then_inc(v_stage, 1)
                wait_apart(pool, v_stage, stage + 3, waited)
                nc.gpsimd.tensor_tensor(rest, rest, part[1], ALU.subtract).then_inc(v_stage, 1)
                wait_apart(pool, v_stage, stage + 4, waited)
                nc.gpsimd.tensor_copy(part[2], rest).then_inc(v_split, 1)

            for i in range(2):
                pool.wait_ge(v_loaded[i], 16)
                split_v(i, i)

            def step(i, u, h, it, last):
                n = step_of(i, h)
                for j in POOL_LO:
                    w = G - P * second[j][2]
                    pool.wait_ge(p_hi_ready, SF0 + NS * n + j + 1)
                    nc.gpsimd.tensor_tensor(p_lo[:, j % RP, :w], prob[:, j % RP, :w], p_hi[:, j % RP, :w], ALU.subtract).then_inc(lo_pool, 1)
                if h == HI - 1 and splits_item(u, last):
                    pool.wait_ge(v_loaded[u], 16 * (it + 2))
                    wait_apart(pool, pv_done, PV0 + NS * (n + 1), waited)
                    split_v(i + 2, u)

            pairs(pool, step)

        @block.scalar
        def _(act):
            act.sem_inc(p_hi_ready, SF0)
            act.wait_ge(id_made, 2)
            nc.scalar.activation(identity_r[:], identity[:], ACT.Copy).then_inc(id_r_made, 1)
            act.wait_ge(aux_loaded, 48)
            for u in range(2):
                for h in range(HI):
                    nc.scalar.activation(qT[AUX:P, u, h], aux_raw[:, 0], ACT.Copy)
                    last = nc.scalar.activation(kT[AUX:P, u, h], aux_raw[:, 1], ACT.Copy)
            last.then_inc(aux_ready, 1)

            def stack_to(k, src, u, h):
                dst = (qT, kT)[k // 2]
                return nc.scalar.activation(dst[0:AUX, u, h, (k % 2) * G:(k % 2 + 1) * G], src, ACT.Copy)

            for h in range(HI):
                for k in range(4):
                    m = 4 * h + k
                    act.wait_ge(misc_full, m + 1)
                    stack_to(k, ps_misc[0:AUX, m % 2], 0, h).then_inc(misc_free, 1)
            act.wait_ge(misc_full, 4 * HI + 1)
            nc.scalar.activation(qT[AUX:P, 0, 0, 0:G], ps_misc[AUX:P, 0], ACT.Copy).then_inc(misc_free, 1)

            def step(i, u, h, it, last):
                n = step_of(i, h)
                stacks = 0
                misc = {}
                for k, (what, j) in enumerate(MISC):
                    misc[j] = (k, what)
                done = 0
                skipped = 0
                for j, (g, kt, t0) in enumerate(second):
                    w = G - P * t0
                    act.wait_ge(second_done, NS * n + j + 1)
                    act.wait_ge(pv_done, PV0 + NS * n + j + 1 - RP)
                    nc.scalar.activation(prob[:, j % RP, :w], ps_second[:, j % 2, :w], ACT.Exp, scale=SCALE).then_inc(prob_ready, 1)
                    nc.scalar.activation(p_hi[:, j % RP, :w], ps_second[:, j % 2, :w], ACT.Exp, scale=SCALE).then_inc(p_hi_ready, 1)
                    if j in misc:
                        k, what = misc[j]
                        if what == "stack" and stacks_item(u, last):
                            act.wait_ge(misc_full, misc_base(n) + k + 1)
                            stack_to(stacks, ps_misc[0:AUX, (k + 1) % 2], 1 - u, h).then_inc(misc_free, 1)
                        elif what == "shift1":
                            act.wait_ge(misc_full, misc_at(i, u, h, last, k) + 1)
                            nc.scalar.activation(qT[AUX:P, u, h, G:2 * G], ps_misc[AUX:P, misc_bank(u, h, last, k)], ACT.Copy).then_inc(misc_free, 1)
                        elif what == "shift0" and has_next_step(u, h, last):
                            u2, h2 = (u, h + 1) if h < HI - 1 else (1 - u, 0)
                            act.wait_ge(misc_full, misc_at(i, u, h, last, k) + 1)
                            nc.scalar.activation(qT[AUX:P, u2, h2, 0:G], ps_misc[AUX:P, misc_bank(u, h, last, k)], ACT.Copy).then_inc(misc_free, 1)
                        stacks += what == "stack"

            def misc_base(n):
                return 4 * HI + 1 + NM * n

            def misc_at(i, u, h, last, k):
                return misc_base(step_of(i, h)) + k if stacks_item(u, last) else misc_base(step_of(ITEMS - 1, 0)) + 2 * h + (k > 0)

            def misc_bank(u, h, last, k):
                return (1 + k) % 2 if stacks_item(u, last) else (1 + (k > 0)) % 2

            pairs(act, step)

        @block.vector
        def _(dve):
            dve.sem_inc(ctx_ready, CF0)
            dve.wait_ge(aux_loaded, 48)
            nc.vector.memset(shiftc[:].bitcast(mybir.dt.uint32), 0).then_inc(zeroed, 1)
            nc.vector.memset(pmax[:], 3e38).then_inc(zeroed, 1)
            dve.wait_ge(zeroed, 2)
            nc.vector.tensor_copy(shiftc[:, :, AUX:MROW], qf_raw[:]).then_inc(shiftc_ready, 1)

            def split_qk(i, u, quarter, m):
                tiles = slice(2 * quarter, 2 * quarter + 2)
                for src, dst, twice in ((q_in, q96, (0, 1)), (k_in, k96, (0, 2))):
                    raw = src[:, u, tiles].rearrange("p t (h d) -> p (t h) d", d=D)
                    out = dst[:, u, tiles].rearrange("p t h (a d) -> p (t h) a d", d=D)
                    both = out[:, :, twice[0]:twice[1] + 1:twice[1] - twice[0], :]
                    nc.vector.tensor_copy(both, raw.unsqueeze(2).broadcast_to([P, 2 * HI, 2, D])).then_inc(hi_made, 1)
                dve.wait_ge(hi_made, 2 * m + 2)
                for src, dst, lo in ((q_in, q96, 2), (k_in, k96, 1)):
                    raw = src[:, u, tiles].rearrange("p t (h d) -> p (t h) d", d=D)
                    out = dst[:, u, tiles].rearrange("p t h (a d) -> p (t h) a d", d=D)
                    last = nc.vector.tensor_tensor(out[:, :, lo], raw, out[:, :, 0].bitcast(F32), ALU.subtract)
                last.then_inc(qk_split, 1)

            for i in range(2):
                dve.wait_ge(q_loaded[i], 16)
                dve.wait_ge(k_loaded[i], 16)
                for c in range(HI):
                    split_qk(i, i, c, HI * i + c)

            def reduce(m, n, j):
                t, k0, w, part = first[j]
                dve.wait_ge(first_done, m + 1)
                out = negmax[:, t:t + 1] if t < GT else pmax[:, t, part:part + 1]
                nc.vector.tensor_reduce(out, ps_first[:, j % 2, :w], AX_X, ALU.max, negate=True).then_inc(first_read, 1)

            def write_shift(n, g):
                tiles = slice(GT * g, GT * (g + 1))
                if g == 0:
                    dve.wait_ge(first_read, NF * n + FG0)
                else:
                    dve.wait_ge(first_read, NF * n + NF)
                    nc.vector.tensor_reduce(negmax[:, tiles], pmax[:, tiles], AX_X, ALU.min).then_inc(negmax_made, 1)
                    dve.wait_ge(negmax_made, n + 1)
                nc.vector.tensor_copy(shiftc[:, tiles, MROW], negmax[:, tiles]).then_inc(shift_hi_made, 1)
                dve.wait_ge(shift_hi_made, 2 * n + g + 1)
                nc.vector.tensor_tensor(shiftc[:, tiles, MROW + 1], negmax[:, tiles], shiftc[:, tiles, MROW].bitcast(F32),
                                        ALU.subtract).then_inc(shift_written, 1)

            for j in range(NF):
                reduce(j, 0, j)
                if j == FG0 - 1:
                    write_shift(0, 0)
            write_shift(0, 1)

            def finish(i, u, h, g, n, it):
                m = NG * n + g
                dve.wait_ge(pv_done, PV0 + NS * n + (GT if g == 0 else NS))
                acc = ps_ctx[:, g, 0:GT * VW].rearrange("p (t w) -> p t w", w=VW)
                nc.vector.tensor_reduce(parts[:, g], acc[:, :, 1:VW].rearrange("p t (a d) -> p t d a", d=D), AX_X, ALU.add)
                nc.vector.reciprocal(recip[:, g], acc[:, :, 0]).then_inc(parts_ready, 1)
                dve.wait_ge(parts_ready, m + 1)
                if h == 0 and g == 0:
                    dve.wait_ge(ctx_stored[u], 16 * (it + 1))
                nc.vector.tensor_tensor(ctx_sb[:, u, GT * g:GT * (g + 1), h * D:(h + 1) * D], parts[:, g],
                                        recip[:, g].unsqueeze(2).broadcast_to([P, GT, D]), ALU.mult).then_inc(ctx_ready, 1)

            def step(i, u, h, it, last):
                n = step_of(i, h)
                nxt = has_next_step(u, h, last)
                for j, (g, kt, t0) in enumerate(second):
                    if nxt:
                        reduce(NF * (n + 1) + j, n + 1, j)
                        if j == FG0 + 1:
                            write_shift(n + 1, 0)
                    if j in DVE_LO:
                        w = G - P * t0
                        dve.wait_ge(p_hi_ready, SF0 + NS * n + j + 1)
                        nc.vector.tensor_tensor(p_lo[:, j % RP, :w], prob[:, j % RP, :w], p_hi[:, j % RP, :w], ALU.subtract).then_inc(lo_dve, 1)
                    if j == GT + LAG + 1:
                        finish(i, u, h, 0, n, it)
                    if j == 9 and splits_item(u, last):
                        if h == 0:
                            dve.wait_ge(q_loaded[u], 16 * (it + 2))
                            dve.wait_ge(k_loaded[u], 16 * (it + 2))
                        split_qk(i + 2, u, h, HI * (i + 2) + h)
                if nxt:
                    write_shift(n + 1, 1)
                finish(i, u, h, 1, n, it)

            pairs(dve, step)

        @block.tensor
        def _(pe):
            def stack(k, bank, u, h):
                src = (q96, k96)[k // 2]
                for t in range(GT):
                    last = nc.tensor.matmul(ps_misc[0:AUX, bank, t * P:(t + 1) * P], src[:, u, (k % 2) * GT + t, h],
                                            identity_r[:], start=True, stop=True)
                last.then_inc(misc_full, 1)

            def shift(g, bank):
                for t in range(GT):
                    last = nc.tensor.matmul(ps_misc[:, bank, t * P:(t + 1) * P], shiftc[:, GT * g + t],
                                            identity_r[:], start=True, stop=True)
                last.then_inc(misc_full, 1)

            def first_pass(u, h, j):
                t, k0, w, part = first[j]
                nc.tensor.matmul(ps_first[:, j % 2, :w], qT[0:MROW, u, h, t * P:(t + 1) * P],
                                 kT[0:MROW, u, h, k0:k0 + w], start=True, stop=True).then_inc(first_done, 1)

            pe.sem_inc(pv_done, PV0)
            pe.wait_ge(id_r_made, 1)
            pe.wait_ge(aux_ready, 1)
            pe.wait_ge(qk_split, HI)
            for h in range(HI):
                for k in range(4):
                    m = 4 * h + k
                    if m >= 2:
                        pe.wait_ge(misc_free, m - 1)
                    stack(k, m % 2, 0, h)
            pe.wait_ge(misc_free, 4)
            for j in range(NF):
                if j >= 2:
                    pe.wait_ge(first_read, j - 1)
                first_pass(0, 0, j)
            pe.wait_ge(shift_written, 1)
            pe.wait_ge(misc_free, 4 * HI - 1)
            shift(0, 0)

            def misc_at(i, u, h, last, k):
                base = 4 * HI + 1 + NM * step_of(i, h)
                return base + k if stacks_item(u, last) else 4 * HI + 1 + NM * step_of(ITEMS - 1, 0) + 2 * h + (k > 0)

            def with_v(n, u, h, j):
                g, kt, t0 = second[j]
                if j in DVE_LO:
                    pe.wait_ge(lo_dve, len(DVE_LO) * n + DVE_LO.index(j) + 1)
                else:
                    pe.wait_ge(lo_pool, len(POOL_LO) * n + POOL_LO.index(j) + 1)
                opening = kt == 0
                if opening:
                    pe.wait_ge(ctx_ready, CF0 + NG * n + g - 1)
                for t in range(t0, GT):
                    cols = slice((t - t0) * P, (t - t0 + 1) * P)
                    nc.tensor.matmul(ps_ctx[:, g, t * VW:(t + 1) * VW], p_hi[:, j % RP, cols], v3[:, u, kt, h],
                                     start=opening and t == 0, stop=False, skip_group_check=True)
                    last = nc.tensor.matmul(ps_ctx[:, g, t * VW:t * VW + 1 + 2 * D], p_lo[:, j % RP, cols],
                                            v3[:, u, kt, h, 0:1 + 2 * D], start=False, stop=False, skip_group_check=True)
                last.then_inc(pv_done, 1)

            def step(i, u, h, it, last):
                n = step_of(i, h)
                nxt = has_next_step(u, h, last)
                u2, h2 = (u, h + 1) if h < HI - 1 else (1 - u, 0)
                misc = {j: (k, what) for k, (what, j) in enumerate(MISC)}
                stacks = 0
                for j, (g, kt, t0) in enumerate(second):
                    w = G - P * t0
                    if j == 0:
                        pe.wait_ge(misc_free, misc_at(i, u, h, last, 0))
                    if kt == 0 and g == 1:
                        pe.wait_ge(misc_free, misc_at(i, u, h, last, 0) + 1)
                    pe.wait_ge(p_hi_ready, SF0 + NS * n + j - 1)
                    nc.tensor.matmul(ps_second[:, j % 2, :w], kT[:, u, h, kt * P:(kt + 1) * P],
                                     qT[:, u, h, g * G + t0 * P:(g + 1) * G], start=True, stop=True).then_inc(second_done, 1)
                    if nxt:
                        if j == 0 and h2 == 0:
                            pe.wait_ge(misc_free, misc_at(i, u, h, last, 0) - 2)
                        pe.wait_ge(first_read, NF * (n + 1) + j - 1)
                        first_pass(u2, h2, j)
                    if j in misc:
                        k, what = misc[j]
                        if what == "stack" and stacks_item(u, last):
                            if h == 0 and stacks == 0:
                                pe.wait_ge(qk_split, HI * (i + 2))
                            pe.wait_ge(misc_free, misc_at(i, u, h, last, k) - 1)
                            stack(stacks, (k + 1) % 2, 1 - u, h)
                        elif what != "stack" and (what == "shift1" or nxt):
                            at = misc_at(i, u, h, last, k)
                            bank = (k + 1) % 2 if stacks_item(u, last) else (1 + (k > 0)) % 2
                            pe.wait_ge(shift_written, 2 * n + (2 if what == "shift1" else 3))
                            pe.wait_ge(misc_free, at - 1)
                            shift(int(what == "shift1"), bank)
                        stacks += what == "stack"
                    if j >= LAG:
                        if j == LAG and h == 0:
                            pe.wait_ge(v_split, i + 1)
                        with_v(n, u, h, j - LAG)
                for j in range(NS - LAG, NS):
                    with_v(n, u, h, j)

            pairs(pe, step)


class Tile:

    def __init__(self, n, u, it, unroll, total):
        self.n, self.u, self.it, self.unroll, self.total = n, u, it, unroll, total

    def shift(self, k):
        v = self.u + k
        return Tile(self.n + k, v % self.unroll, self.it + v // self.unroll, self.unroll, self.total)

    @property
    def real(self):
        return not isinstance(self.n, int) or 0 <= self.n < self.total

    def at_least(self, k):
        return not isinstance(self.n, int) or self.n >= k


def pipelined(eng, total, unroll, before, after, step):
    head = range(-before, unroll)
    tail = range(total - unroll, total + after)
    for n in head:
        step(Tile(n, n % unroll, n // unroll, unroll, total))
    with eng.Fori(1, total // unroll - 1) as it:
        for u in range(unroll):
            step(Tile(unroll * it + u, u, it, unroll, total))
    for n in tail:
        step(Tile(n, n % unroll, n // unroll, unroll, total))


def mix_phase(nc, ctx_rows, x, w_o, w_ra, b_r, iota8, x1_rows, xnT_cols, zm_cols, w_rows, w_sum):
    N, C = x.shape
    NT, CT = N // P, C // P
    E, R = 8, 8
    ER = E * R
    RW = ER + E
    BT = 4
    ZF0, MR0 = 4, 1
    LINKS = 19

    with Space(nc, "c_") as s:
        identity = s.sb("identity", [P, P])
        w_raw = s.sb("w_raw", [P, CT, C])
        w = s.sb("w", [P, 2, CT, C], F32R)
        wr_raw = s.sb("wr_raw", [P, CT, RW])
        wr = s.sb("wr", [P, 2, CT, RW], F32R)
        br_sb = s.sb("br_sb", [P, E])
        iota_sb = s.sb("iota_sb", [P, E])
        norm_consts = s.sb("norm_consts", [P, 3])
        ctx_in = s.sb("ctx_in", [P, 2, C])
        x_in = s.sb("x_in", [P, 2, C])
        cT = s.sb("cT", [P, 2, 2, CT, P], F32R)
        attn = s.sb("attn", [P, 2, C])
        x1 = s.sb("x1", [P, 2, C])
        xn = s.sb("xn", [P, 2, C])
        xnT = s.sb("xnT", [P, 2, 2, CT, P], F32R)
        stats = s.sb("stats", [P, 2, 2, 6])
        mean_var = s.sb("mean_var", [P, 2, 2, 2])
        coef = s.sb("coef", [P, 2, 2, 4])
        u1 = s.sb("u1", [P, BT, ER])
        small = {k: s.sb(k, [P, BT, E]) for k in ("logits", "centred", "expd", "probs", "equal", "cand", "hot1", "rest", "hot2", "twice1", "twice2", "delta")}
        one = {k: s.sb(k, [P, BT]) for k in ("top", "total", "recip", "w1", "first1", "w2", "first2")}
        z = s.sb("z", [P, 2, BT, ER])
        zs = s.sb("zs", [P, 2, BT, P], F32R)
        masks = s.sb("masks", [P, 2, BT, P])
        w_cols = s.sb("w_cols", [P, BT, P])
        zT = s.sb("zT", [P, 2, 4, P])
        wT = s.sb("wT", [2, 2, P])
        ps_cT = s.ps("ps_cT", [P, CT, P])
        ps_o = s.ps("ps_o", [P, 2, C])
        ps_xT = s.ps("ps_xT", [P, CT, P])
        ps_r = s.ps("ps_r", [P, 512])
        ps_z = s.ps("ps_z", [P, 2, 4, P])
        ps_w = s.ps("ps_w", [P, 512])
        rr = ps_r[:, 0:BT * RW].rearrange("p (t r) -> p t r", r=RW)

        id_made, norm_consts_made, cols_zeroed = s.sem("id_made"), s.sem("norm_consts_made"), s.sem("cols_zeroed")
        w_loaded, consts_loaded = s.sem("w_loaded"), s.sem("consts_loaded")
        w_hi, w_lo = s.sem("w_hi"), s.sem("w_lo")
        ctx_loaded, x_loaded = s.sems("ctx_loaded", 2), s.sems("x_loaded", 2)
        cT_in_psum, cT_hi, cT_lo = s.sem("cT_in_psum"), s.sem("cT_hi"), s.sem("cT_lo")
        o_done = s.sem("o_done")
        bn, stats_ready, eps_added, rstd_ready, shift_ready = (s.sems(k, 2) for k in ("bn", "stats", "eps", "rstd_r", "shift_r"))
        attn_ready, x1_ready, xn_ready = s.sem("attn_ready"), s.sem("x1_ready"), s.sem("xn_ready")
        x1_stored, xnT_stored = s.sems("x1_stored", 2), s.sems("xnT_stored", 2)
        xT_in_psum, xT_hi, xT_lo = s.sem("xT_in_psum"), s.sem("xT_hi"), s.sem("xT_lo")
        r_done, r_read = s.sem("r_done"), s.sem("r_read")
        chain = s.sem("chain")
        centred_ready, exp_ready = s.sem("centred_ready"), s.sem("exp_ready")
        hots_ready, masks_ready, z_ready = s.sem("hots_ready"), s.sem("masks_ready"), s.sem("z_ready")
        z_in_psum, z_out = s.sem("z_in_psum"), s.sem("z_out")
        z_stored, wT_stored = s.sems("z_stored", 2), s.sems("wT_stored", 2)
        waited = s.sem("waited")
        block = s.block()
        STAGES = dict(total=NT, unroll=4, before=2, after=6)

        def batch_of(t):
            b = t.it - 1
            ok = not isinstance(b, int) or 0 <= b < NT // BT
            return b if ok else None

        @block.sync
        def _(sp):
            for u in range(2):
                sp.sem_inc(z_stored[u], 16)
                sp.sem_inc(wT_stored[u], 16)
            sp.dma_start(w_raw[:], w_o.rearrange("(c p) o -> p c o", p=P)).then_inc(w_loaded, 16)
            sp.dma_start(wr_raw[:], w_ra.rearrange("(c p) o -> p c o", p=P)).then_inc(w_loaded, 16)
            sp.dma_start(br_sb[:], b_r.partition_broadcast(P)).then_inc(consts_loaded, 16)
            sp.dma_start(iota_sb[:], iota8.partition_broadcast(P)).then_inc(consts_loaded, 16)

            def step(t):
                a = t.shift(2)
                if a.real:
                    if a.at_least(2):
                        sp.wait_ge(cT_in_psum, a.n - 1)
                    sp.dma_start(ctx_in[:, a.u % 2], ctx_rows[bass.ds(a.n * P, P), :]).then_inc(ctx_loaded[a.u % 2], 16)
                b = t.shift(1)
                if b.real:
                    if b.at_least(2):
                        sp.wait_ge(x1_ready, b.n - 1)
                    sp.dma_start(x_in[:, b.u % 2], x[bass.ds(b.n * P, P), :]).then_inc(x_loaded[b.u % 2], 16)
                c = t.shift(-1)
                if c.real:
                    sp.wait_ge(x1_ready, c.n + 1)
                    sp.dma_start(x1_rows[bass.ds(c.n * P, P), :], x1[:, c.u % 2]).then_inc(x1_stored[c.u % 2], 16)
                    wait_apart(sp, xT_lo, c.n + 1, waited)
                    for a_ in range(2):
                        sp.dma_start(xnT_cols[:, a_, :, bass.ds(c.n * P, P)], xnT[:, c.u % 2, a_].bitcast(F32)).then_inc(xnT_stored[c.u % 2], 16)
                b = batch_of(t)
                if b is not None and t.u == 3:
                    for k in range(BT):
                        m = b * BT + k
                        sp.wait_ge(z_out, ZF0 + 2 * m + 2)
                        sp.dma_start(zm_cols[:, :, bass.ds(m * P, P)], zT[:, k % 2]).then_inc(z_stored[k % 2], 16)
                        sp.dma_start(w_rows[:, bass.ds(m * P, P)], wT[:, k % 2]).then_inc(wT_stored[k % 2], 16)

            pipelined(sp, step=step, **STAGES)
            for u in range(2):
                sp.wait_ge(x1_stored[u], 16 * (NT // 2))
                sp.wait_ge(xnT_stored[u], 32 * (NT // 2))
                sp.wait_ge(z_stored[u], 16 * (NT // 2 + 1))
                sp.wait_ge(wT_stored[u], 16 * (NT // 2 + 1))

        def slot_uses(t, per=16):
            return per * (2 * t.it + t.u // 2)

        @block.gpsimd
        def _(pool):
            make_identity(nc, pool, identity, id_made)
            pool.sem_inc(masks_ready, MR0)
            nc.gpsimd.memset(w_cols[:], 0.0).then_inc(cols_zeroed, 1)
            make_norm_constants(nc, pool, norm_consts, norm_consts_made)

            def coefficients(j, t):
                layer_norm_coefficients(nc, pool, norm_consts, mean_var[:, j, t.u % 2], coef[:, j, t.u % 2],
                                        stats_ready[j], eps_added[j], rstd_ready[j], shift_ready[j], t.n + 1)

            def step(t):
                b = batch_of(t)
                if b is not None and t.u == 3:
                    pool.wait_ge(hots_ready, b + 1)
                    wait_apart(pool, z_out, ZF0 + 2 * BT * b, waited)
                    for k, name in enumerate(("twice1", "twice2")):
                        src = small[name][:].unsqueeze(3).broadcast_to([P, BT, E, R])
                        for c in range(2):
                            last = nc.gpsimd.tensor_copy(masks[:, k, :, c * ER:(c + 1) * ER].rearrange("p t (e r) -> p t e r", r=R), src)
                    last.then_inc(masks_ready, 1)
                if t.real:
                    u = t.u % 2
                    coefficients(0, t)
                    pool.wait_ge(attn_ready, t.n + 1)
                    if t.at_least(2):
                        pool.wait_ge(x1_stored[u], slot_uses(t))
                        pool.wait_ge(xn_ready, t.n - 1)
                    pool.wait_ge(x_loaded[u], slot_uses(t) + 16)
                    nc.gpsimd.tensor_tensor(x1[:, u], x_in[:, u], attn[:, u], ALU.add).then_inc(x1_ready, 1)
                    coefficients(1, t)

            pipelined(pool, step=step, **STAGES)

        @block.scalar
        def _(act):
            act.sem_inc(z_out, ZF0)
            act.wait_ge(w_loaded, 32)
            nc.scalar.activation(w[:, 0], w_raw[:], ACT.Copy)
            nc.scalar.activation(wr[:, 0], wr_raw[:], ACT.Copy).then_inc(w_hi, 1)

            def step(t):
                a = t.shift(1)
                if a.real:
                    act.wait_ge(cT_in_psum, a.n + 1)
                    if a.at_least(2):
                        act.wait_ge(o_done, a.n - 1)
                    nc.scalar.activation(cT[:, a.u % 2, 0], ps_cT[:], ACT.Copy).then_inc(cT_hi, 1)
                c = t.shift(-1)
                if c.real:
                    act.wait_ge(xT_in_psum, c.n + 1)
                    if c.at_least(2):
                        act.wait_ge(r_done, c.n - 1)
                        act.wait_ge(xnT_stored[c.u % 2], slot_uses(c, 32))
                    nc.scalar.activation(xnT[:, c.u % 2, 0], ps_xT[:], ACT.Copy).then_inc(xT_hi, 1)
                if t.real:
                    u = t.u % 2
                    act.wait_ge(shift_ready[0], t.n + 1)
                    if t.at_least(2):
                        act.wait_ge(x1_ready, t.n - 1)
                    nc.scalar.activation(attn[:, u], ps_o[:, u], ACT.Identity, bias=coef[:, 0, u, 3:4],
                                         scale=coef[:, 0, u, 2:3]).then_inc(attn_ready, 1)
                b = batch_of(t)
                if b is not None and t.u == 1:
                    act.wait_ge(centred_ready, b + 1)
                    nc.scalar.activation(small["expd"][:], small["centred"][:], ACT.Exp).then_inc(exp_ready, 1)
                if t.real:
                    act.wait_ge(shift_ready[1], t.n + 1)
                    if t.at_least(2):
                        act.wait_ge(xT_in_psum, t.n - 1)
                    nc.scalar.activation(xn[:, u], x1[:, u], ACT.Identity, bias=coef[:, 1, u, 3:4],
                                         scale=coef[:, 1, u, 2:3]).then_inc(xn_ready, 1)
                if b is not None and t.u == 3:
                    for k in range(BT):
                        m = b * BT + k
                        act.wait_ge(z_in_psum, 2 * m + 1)
                        act.wait_ge(z_stored[k % 2], 16 * (2 * b + k // 2 + 1))
                        act.wait_ge(wT_stored[k % 2], 16 * (2 * b + k // 2 + 1))
                        nc.scalar.activation(zT[:, k % 2], ps_z[:, k % 2], ACT.Copy).then_inc(z_out, 1)
                        act.wait_ge(z_in_psum, 2 * m + 2)
                        nc.scalar.activation(wT[:, k % 2], ps_w[0:2, 0:P], ACT.Copy).then_inc(z_out, 1)

            pipelined(act, step=step, **STAGES)

        @block.vector
        def _(dve):
            dve.wait_ge(w_hi, 1)
            nc.vector.tensor_tensor(w[:, 1], w_raw[:], w[:, 0].bitcast(F32), ALU.subtract)
            nc.vector.tensor_tensor(wr[:, 1], wr_raw[:], wr[:, 0].bitcast(F32), ALU.subtract).then_inc(w_lo, 1)
            dve.wait_ge(consts_loaded, 32)
            dve.wait_ge(cols_zeroed, 1)

            def statistics(j, t, src):
                u = t.u % 2
                nc.vector.bn_stats(stats[:, j, u], src).then_inc(bn[j], 1)
                wait_apart(dve, bn[j], t.n + 1, waited)
                nc.vector.bn_aggr(mean_var[:, j, u], stats[:, j, u]).then_inc(stats_ready[j], 1)


            def route(b, part):
                links = [0 if part == 0 else 2]

                def link(ins):
                    links[0] += 1
                    ins.then_inc(chain, 1)
                    dve.wait_ge(chain, LINKS * b + links[0])

                V, S, O = nc.vector, small, one

                def wide(v):
                    return v[:].unsqueeze(2).broadcast_to([P, BT, E])

                iota = iota_sb[:].unsqueeze(1).broadcast_to([P, BT, E])
                if part == 0:
                    dve.wait_ge(r_done, BT * (b + 1))
                    V.tensor_copy(u1[:], rr[:, :, 0:ER])
                    link(V.tensor_tensor(S["logits"][:], rr[:, :, ER:RW], br_sb[:].unsqueeze(1).broadcast_to([P, BT, E]), ALU.add))
                    link(V.tensor_reduce(O["top"][:], S["logits"][:], AX_X, ALU.max))
                    V.tensor_tensor(S["centred"][:], S["logits"][:], wide(O["top"]), ALU.subtract).then_inc(centred_ready, 1)
                    return
                dve.wait_ge(exp_ready, b + 1)
                link(V.tensor_reduce(O["total"][:], S["expd"][:], AX_X, ALU.add))
                link(V.reciprocal(O["recip"][:], O["total"][:]))
                link(V.tensor_tensor(S["probs"][:], S["expd"][:], wide(O["recip"]), ALU.mult))
                for src, wt, first, hot in (("probs", "w1", "first1", "hot1"), ("rest", "w2", "first2", "hot2")):
                    link(V.tensor_reduce(O[wt][:], S[src][:], AX_X, ALU.max))
                    link(V.tensor_tensor(S["equal"][:], S[src][:], wide(O[wt]), ALU.is_equal))
                    link(V.tensor_tensor(S["cand"][:], S["equal"][:], iota, ALU.mult))
                    link(V.tensor_reduce(O[first][:], S["cand"][:], AX_X, ALU.min))
                    link(V.tensor_tensor(S[hot][:], iota, wide(O[first]), ALU.is_equal))
                    if hot == "hot1":
                        link(V.scalar_tensor_tensor(S["rest"][:], S["hot1"][:], -2.0, S["probs"][:], ALU.mult, ALU.add))
                dve.wait_ge(masks_ready, MR0 + b)
                dve.wait_ge(z_out, ZF0 + 2 * BT * b)
                V.tensor_scalar(S["twice1"][:], S["hot1"][:], 2.0, None, ALU.mult)
                link(V.tensor_scalar(S["twice2"][:], S["hot2"][:], 2.0, None, ALU.mult))
                V.tensor_copy(w_cols[:, :, 0], O["w1"][:])
                V.tensor_copy(w_cols[:, :, 1], O["w2"][:])
                V.tensor_tensor(w_sum[:, bass.ds(b * BT, BT)], O["w1"][:], O["w2"][:], ALU.add)
                V.tensor_tensor(S["delta"][:], S["twice2"][:], S["twice1"][:], ALU.subtract).then_inc(hots_ready, 1)
                dve.wait_ge(hots_ready, b + 1)
                for k, name in enumerate(("twice1", "delta")):
                    last = V.tensor_tensor(z[:, k].rearrange("p t (e r) -> p (t e) r", r=R), u1[:].rearrange("p t (e r) -> p (t e) r", r=R),
                                           S[name][:].rearrange("p t e -> p (t e)").unsqueeze(2).broadcast_to([P, BT * E, R]), ALU.mult)
                link(last)
                link(V.tensor_copy(zs[:, :, :, 0:ER], z[:]))
                V.tensor_tensor(zs[:, :, :, ER:2 * ER], z[:], zs[:, :, :, 0:ER].bitcast(F32), ALU.subtract).then_inc(z_ready, 1)
                assert links[0] == LINKS, links

            def step(t):
                a = t.shift(1)
                if a.real:
                    dve.wait_ge(cT_hi, a.n + 1)
                    nc.vector.tensor_tensor(cT[:, a.u % 2, 1], ps_cT[:], cT[:, a.u % 2, 0].bitcast(F32), ALU.subtract).then_inc(cT_lo, 1)
                b = batch_of(t)
                if b is not None and t.u == 1:
                    route(b, 0)
                c = t.shift(-1)
                if c.real:
                    dve.wait_ge(xT_hi, c.n + 1)
                    nc.vector.tensor_tensor(xnT[:, c.u % 2, 1], ps_xT[:], xnT[:, c.u % 2, 0].bitcast(F32), ALU.subtract).then_inc(xT_lo, 1)
                if t.real:
                    dve.wait_ge(o_done, t.n + 1)
                    statistics(0, t, ps_o[:, t.u % 2])
                if b is not None and t.u == 2:
                    route(b, 1)
                if t.real:
                    dve.wait_ge(x1_ready, t.n + 1)
                    statistics(1, t, x1[:, t.u % 2])

            pipelined(dve, step=step, **STAGES)

        @block.tensor
        def _(pe):
            pe.wait_ge(id_made, 2)

            def step(t):
                a = t.shift(1)
                if a.real:
                    u = a.u % 2
                    pe.wait_ge(ctx_loaded[u], slot_uses(a) + 16)
                    if a.at_least(1):
                        pe.wait_ge(cT_lo, a.n)
                    for c in range(CT):
                        last = nc.tensor.transpose(ps_cT[:, c], ctx_in[:, u, c * P:(c + 1) * P], identity[:])
                    last.then_inc(cT_in_psum, 1)
                if t.real:
                    u = t.u % 2
                    if isinstance(t.n, int) and t.n == 0:
                        pe.wait_ge(w_lo, 1)
                    pe.wait_ge(cT_lo, t.n + 1)
                    if t.at_least(2):
                        pe.wait_ge(attn_ready, t.n - 1)
                    k = 0
                    for c in range(CT):
                        for x_, w_ in SPLIT_PAIRS:
                            last = nc.tensor.matmul(ps_o[:, u], cT[:, u, x_, c], w[:, w_, c], start=k == 0, stop=k == 3 * CT - 1)
                            k += 1
                    last.then_inc(o_done, 1)
                c = t.shift(-1)
                if c.real:
                    u = c.u % 2
                    pe.wait_ge(xn_ready, c.n + 1)
                    if c.at_least(1):
                        pe.wait_ge(xT_lo, c.n)
                    for k in range(CT):
                        last = nc.tensor.transpose(ps_xT[:, k], xn[:, u, k * P:(k + 1) * P], identity[:])
                    last.then_inc(xT_in_psum, 1)
                    pe.wait_ge(xT_lo, c.n + 1)
                    if c.u == 0 and c.at_least(1):
                        pe.wait_ge(chain, LINKS * (c.it - 1) + 1)
                    k = 0
                    for q in range(CT):
                        for x_, w_ in SPLIT_PAIRS:
                            last = nc.tensor.matmul(rr[:, c.u], xnT[:, u, x_, q], wr[:, w_, q], start=k == 0, stop=k == 3 * CT - 1)
                            k += 1
                    last.then_inc(r_done, 1)
                b = batch_of(t)
                if b is not None and t.u == 3:
                    pe.wait_ge(z_ready, b + 1)
                    pe.wait_ge(masks_ready, MR0 + b + 1)
                    for k in range(BT):
                        m = b * BT + k
                        pe.wait_ge(z_out, ZF0 + 2 * m - 3)
                        srcs = [zs[:, 0, k].bitcast(F32), zs[:, 1, k].bitcast(F32), masks[:, 0, k], masks[:, 1, k]]
                        for q, src in enumerate(srcs):
                            last = nc.tensor.transpose(ps_z[:, k % 2, q], src, identity[:])
                        last.then_inc(z_in_psum, 1)
                        pe.wait_ge(z_out, ZF0 + 2 * m)
                        nc.tensor.transpose(ps_w[:, 0:P], w_cols[:, k], identity[:]).then_inc(z_in_psum, 1)

            pipelined(pe, step=step, **STAGES)


class ExpertWeights:

    def __init__(self, s, C, F, ER):
        CT, FT = C // P, F // P
        self.w1 = s.sb("w1", [P, 2, CT, F], F32R)
        self.w2 = s.sb("w2", [P, 2, FT, C], F32R)
        self.a2 = s.sb("a2", [P, FT, 2 * ER], F32R)
        self.b1 = s.sb("b1", [P, F], F32R)
        self.ER = ER
        self.b2 = s.sb("b2", [P, 2, C], F32R)


def load_experts(nc, wts, w1, w2, a2, b1, b2):
    C, F = w1.shape
    ER = a2.shape[1]
    CT, FT = C // P, F // P
    with Space(nc, "d_") as s:
        BUFS = 4
        raw = s.sb("raw", [P, BUFS, 2048])
        loaded = s.sems("loaded", BUFS)
        hi_ready, lo_ready = s.sem("hi_ready"), s.sem("lo_ready")
        jobs = []
        w1v, w2v = w1.rearrange("(c p) f -> p c f", p=P), w2.rearrange("(t p) o -> p t o", p=P)
        for c in range(CT):
            jobs.append(([(slice(0, P), w1v[:, c])], wts.w1[:, 0, c], wts.w1[:, 1, c], lambda r: r))
        for t in range(0, FT, 4):
            jobs.append(([(slice(0, P), w2v[:, t:t + 4])], wts.w2[:, 0, t:t + 4], wts.w2[:, 1, t:t + 4],
                         lambda r: r.rearrange("p (t o) -> p t o", t=4)))
        jobs.append(([(slice(0, P), a2.rearrange("(t p) e -> p t e", p=P))], wts.a2[:, :, 0:ER], wts.a2[:, :, ER:2 * ER],
                     lambda r: r[:, 0:FT * ER].rearrange("p (t e) -> p t e", t=FT)))
        jobs.append(([(slice(0, ER), b1), (slice(ER, 2 * ER), b1)], wts.b1[:], wts.b1[ER:2 * ER], lambda r: r))
        jobs.append(([(slice(0, ER), b2), (slice(ER, 2 * ER), b2)], wts.b2[:, 0], wts.b2[:, 1], lambda r: r[:, 0:C]))
        landed, count = [], [0] * BUFS
        for k, (dmas, *_) in enumerate(jobs):
            count[k % BUFS] += 16 * len(dmas)
            landed.append(count[k % BUFS])
        block = s.block()

        @block.sync
        def _(sp):
            for k, (dmas, hi, lo, view) in enumerate(jobs):
                if k >= BUFS:
                    sp.wait_ge(lo_ready, k - BUFS + 1)
                for rows, src in dmas:
                    sp.dma_start(view(raw[:, k % BUFS])[rows], src).then_inc(loaded[k % BUFS], 16)

        @block.scalar
        def _(act):
            for k, (dmas, hi, lo, view) in enumerate(jobs):
                act.wait_ge(loaded[k % BUFS], landed[k])
                nc.scalar.activation(hi, view(raw[:, k % BUFS]), ACT.Copy).then_inc(hi_ready, 1)

        @block.vector
        def _(dve):
            for k, (dmas, hi, lo, view) in enumerate(jobs):
                rows = slice(P - lo.shape[0], P)
                dve.wait_ge(hi_ready, k + 1)
                nc.vector.tensor_tensor(lo, view(raw[:, k % BUFS])[rows], hi[rows].bitcast(F32), ALU.subtract).then_inc(lo_ready, 1)


def expert_phase(nc, wts, xnT_cols, zm_cols, w_rows, w_sum, x1_rows, b1_cols, b2_row, out):
    N, C = out.shape
    CT, FT = C // P, wts.w2.shape[2]
    G = 256
    NG, GT = N // G, G // P
    ER = wts.ER
    RH = 2

    with Space(nc, "e_") as s:
        b1_sb = s.sb("b1_sb", [P, FT])
        b2_sb = s.sb("b2_sb", [P, C])
        norm_consts = s.sb("norm_consts", [P, 3])
        xT = s.sb("xT", [P, 2, 2, CT, G], F32R)
        z_hi = s.sb("z_hi", [P, 2, 2, G], F32R)
        z_lo = s.sb("z_lo", [ER, 2, 2, G], F32R)
        masks = s.sb("masks", [P, 2, G])
        wk = s.sb("wk", [P, 2, 2, G])
        h = s.sb("h", [P, 2, 3, G])
        h_hi = s.sb("h_hi", [P, 2, 3, G], F32R)
        h_lo = s.sb("h_lo", [P, 2, 3, G], F32R)
        z2 = s.sb("z2", [P, 2, G])
        z2s = s.sb("z2s", [P, 2, G], F32R)
        y = s.sb("y", [P, C])
        x1_in = s.sb("x1_in", [P, C])
        stats = s.sb("stats", [P, 6])
        mean_var = s.sb("mean_var", [P, 2])
        coef = s.sb("coef", [P, 4])
        ps_h = s.ps("ps_h", [P, RH, 512])
        ps_u = s.ps("ps_u", [P, 2, G])
        ps_y = s.ps("ps_y", [P, 2, GT, C])

        norm_consts_made = s.sem("norm_consts_made")
        consts_loaded = s.sem("consts_loaded")
        x_loaded, z_loaded, wk_loaded = s.sems("x_loaded", 2), s.sems("z_loaded", 2), s.sems("wk_loaded", 2)
        masks_loaded = s.sem("masks_loaded")
        x1_loaded = s.sem("x1_loaded")
        base_done, moved_done = s.sem("base_done"), s.sem("moved_done")
        h0_ready, h1_ready = s.sem("h0_ready"), s.sem("h1_ready")
        g_ready, hi_ready, lo_ready = s.sem("g_ready"), s.sem("hi_ready"), s.sem("lo_ready")
        used = s.sem("used")
        masked, z2_sum, z2_hi, z2_ready = s.sem("masked"), s.sem("z2_sum"), s.sem("z2_hi"), s.sem("z2_ready")
        y_done, y_ready = s.sem("y_done"), s.sem("y_ready")
        bn, stats_ready, eps_added, rstd_ready, shift_ready = (s.sem(k) for k in ("bn", "stats_r", "eps", "rstd_r", "shift_r"))
        y_normed, out_ready = s.sem("y_normed"), s.sem("out_ready")
        out_stored = s.sem("out_stored")
        waited = s.sem("waited")
        block = s.block()

        STAGES = dict(total=NG, unroll=2, before=0, after=1)

        def bank(t, f):
            return f % 2

        def F(t, f):
            return FT * t.n + f

        @block.sync
        def _(sp):
            sp.dma_start(b1_sb[:], b1_cols).then_inc(consts_loaded, 16)
            sp.dma_start(b2_sb[:], b2_row.partition_broadcast(P)).then_inc(consts_loaded, 16)

            def load(t):
                u, cols = t.u, bass.ds(t.n * G, G)
                for a in range(2):
                    sp.dma_start(xT[:, u, a].bitcast(F32), xnT_cols[:, a, :, cols]).then_inc(x_loaded[u], 16)
                for dst, src in ((z_hi[0:ER, u], 0), (z_hi[ER:2 * ER, u], 0), (z_lo[:, u], ER)):
                    sp.dma_start(dst.bitcast(F32), zm_cols[src:src + ER, 0:2, cols]).then_inc(z_loaded[u], 16)
                for k in range(2):
                    sp.dma_start(wk[:, u, k], w_rows[k, cols].partition_broadcast(P)).then_inc(wk_loaded[u], 16)

            def step(t):
                if isinstance(t.n, int) and t.n == 0:
                    load(t)
                n = t.shift(1)
                if n.real and t.real:
                    if n.at_least(2):
                        sp.wait_ge(used, F(t, 0))
                    load(n)
                if t.real:
                    if t.at_least(1):
                        sp.wait_ge(masked, t.n)
                    sp.dma_start(masks[:], zm_cols[:, 2:4, bass.ds(t.n * G, G)]).then_inc(masks_loaded, 16)
                p = t.shift(-1)
                if p.real:
                    for j in range(GT):
                        m = GT * p.n + j
                        if not (isinstance(p.n, int) and p.n == 0 and j == 0):
                            sp.wait_ge(out_stored, 16 * m)
                        rows = bass.ds((GT * p.n + j) * P, P)
                        sp.dma_start(x1_in[:], x1_rows[rows, :]).then_inc(x1_loaded, 16)
                        sp.wait_ge(out_ready, m + 1)
                        sp.dma_start(out[rows, :], x1_in[:]).then_inc(out_stored, 16)

            pipelined(sp, step=step, **STAGES)
            sp.wait_ge(out_stored, 16 * NG * GT)

        @block.gpsimd
        def _(pool):
            make_norm_constants(nc, pool, norm_consts, norm_consts_made)

            def step(t):
                p = t.shift(-1)
                if p.real:
                    for j in range(GT):
                        m = GT * p.n + j
                        layer_norm_coefficients(nc, pool, norm_consts, mean_var, coef,
                                                stats_ready, eps_added, rstd_ready, shift_ready, m + 1)
                        pool.wait_ge(y_normed, m + 1)
                        pool.wait_ge(x1_loaded, 16 * (m + 1))
                        nc.gpsimd.tensor_tensor(x1_in[:], x1_in[:], y[:], ALU.add).then_inc(out_ready, 1)

            pipelined(pool, step=step, **STAGES)

        @block.scalar
        def _(act):
            act.wait_ge(consts_loaded, 32)

            def gelu(t, f, k):
                n = F(t, f)
                act.wait_ge((base_done, moved_done)[k], n + 1)
                if not (isinstance(n, int) and n < 2):
                    act.wait_ge(lo_ready, 3 * (n - 1))
                nc.scalar.activation(h[:, f % 2, k], ps_h[:, bank(t, f), 0:G], ACT.Gelu_apprx_tanh,
                                     bias=b1_sb[:, f:f + 1]).then_inc((h0_ready, h1_ready)[k], 1)

            def step(t):
                p = t.shift(-1)
                for f in range(FT):
                    if t.real:
                        gelu(t, f, 0)
                        gelu(t, f, 1)
                    if p.real and f in (4, 8):
                        m = GT * p.n + (f == 8)
                        act.wait_ge(shift_ready, m + 1)
                        nc.scalar.activation(y[:], y[:], ACT.Identity, bias=coef[:, 3:4], scale=coef[:, 2:3]).then_inc(y_normed, 1)

            pipelined(act, step=step, **STAGES)

        @block.vector
        def _(dve):
            def scale(t, f):
                n, b = F(t, f), f % 2
                V = nc.vector
                if f == 0:
                    dve.wait_ge(wk_loaded[t.u], 32 * (t.it + 1))
                for k in range(2):
                    dve.wait_ge((h0_ready, h1_ready)[k], n + 1)
                    V.tensor_tensor(h[:, f % 2, k], h[:, f % 2, k], wk[:, t.u, k], ALU.mult).then_inc(g_ready, 1)
                if not (isinstance(n, int) and n < 2):
                    dve.wait_ge(used, n - 1)
                dve.wait_ge(g_ready, 3 * n + 2)
                V.tensor_tensor(h[:, f % 2, 2], h[:, f % 2, 0], h[:, f % 2, 1], ALU.add).then_inc(g_ready, 1)
                V.tensor_copy(h_hi[:, b, 0:2], h[:, f % 2, 0:2]).then_inc(hi_ready, 1)
                dve.wait_ge(g_ready, 3 * n + 3)
                V.tensor_copy(h_hi[:, b, 2], h[:, f % 2, 2]).then_inc(hi_ready, 1)
                dve.wait_ge(hi_ready, 2 * n + 1)
                V.tensor_tensor(h_lo[:, b, 0:2], h[:, f % 2, 0:2], h_hi[:, b, 0:2].bitcast(F32), ALU.subtract).then_inc(lo_ready, 2)
                dve.wait_ge(hi_ready, 2 * n + 2)
                V.tensor_tensor(h_lo[:, b, 2], h[:, f % 2, 2], h_hi[:, b, 2].bitcast(F32), ALU.subtract).then_inc(lo_ready, 1)

            def mask(p):
                V = nc.vector
                dve.wait_ge(used, F(p, FT))
                dve.wait_ge(masks_loaded, 16 * (p.n + 1))
                for k in range(2):
                    last = V.tensor_tensor(z2[:, k], ps_u[:, k], masks[:, k], ALU.mult)
                last.then_inc(masked, 1)
                dve.wait_ge(masked, p.n + 1)
                V.tensor_tensor(z2[:, 0], z2[:, 0], z2[:, 1], ALU.add).then_inc(z2_sum, 1)
                dve.wait_ge(z2_sum, p.n + 1)
                if p.at_least(1):
                    dve.wait_ge(y_done, GT * p.n)
                V.tensor_copy(z2s[:, 0], z2[:, 0]).then_inc(z2_hi, 1)
                dve.wait_ge(z2_hi, p.n + 1)
                V.tensor_tensor(z2s[:, 1], z2[:, 0], z2s[:, 0].bitcast(F32), ALU.subtract).then_inc(z2_ready, 1)

            def close(p, j):
                m = GT * p.n + j
                V = nc.vector
                dve.wait_ge(y_done, m + 1)
                if not (isinstance(m, int) and m == 0):
                    dve.wait_ge(out_ready, m)
                V.scalar_tensor_tensor(y[:], b2_sb[:], w_sum[:, bass.ds(m, 1)], ps_y[:, p.u, j], ALU.mult, ALU.add).then_inc(y_ready, 1)
                dve.wait_ge(y_ready, m + 1)
                V.bn_stats(stats[:], y[:]).then_inc(bn, 1)
                wait_apart(dve, bn, m + 1, waited)
                V.bn_aggr(mean_var[:], stats[:]).then_inc(stats_ready, 1)

            def step(t):
                p = t.shift(-1)
                for f in range(FT):
                    if p.real and f == 0:
                        mask(p)
                    if t.real:
                        scale(t, f)
                    if p.real and f in (3, 7):
                        close(p, int(f == 7))

            dve.wait_ge(consts_loaded, 32)
            pipelined(dve, step=step, **STAGES)

        @block.tensor
        def _(pe):
            def base(t, f):
                u, n, b = t.u, F(t, f), bank(t, f)
                if f == 0:
                    pe.wait_ge(x_loaded[u], 32 * (t.it + 1))
                    pe.wait_ge(z_loaded[u], 48 * (t.it + 1))
                if not (isinstance(n, int) and n < 2):
                    pe.wait_ge(h1_ready, n - 1)
                cols = slice(f * P, (f + 1) * P)
                first = True
                for c in range(CT):
                    for x_, w_ in SPLIT_PAIRS:
                        nc.tensor.matmul(ps_h[:, b, 0:G], wts.w1[:, w_, c, cols], xT[:, u, x_, c], start=first, stop=False,
                                         skip_group_check=True)
                        first = False
                low_rank(t, f, 0).then_inc(base_done, 1)

            def low_rank(t, f, k):
                cols = slice(f * P, (f + 1) * P)
                dst = ps_h[:, bank(t, f), 0:G]
                nc.tensor.matmul(dst, wts.b1[0:ER, cols], z_lo[:, t.u, k], start=False, stop=False, skip_group_check=True)
                return nc.tensor.matmul(dst, wts.b1[:, cols], z_hi[:, t.u, k], start=False, stop=False, skip_group_check=True)

            def moved(t, f):
                pe.wait_ge(h0_ready, F(t, f) + 1)
                low_rank(t, f, 1).then_inc(moved_done, 1)

            def down(t, f):
                n, b = F(t, f), f % 2
                pe.wait_ge(lo_ready, 3 * n + 3)
                if f == 0 and t.at_least(1):
                    pe.wait_ge(masked, t.n)
                for k in range(2):
                    for q, part in enumerate((h_hi, h_lo)):
                        nc.tensor.matmul(ps_u[:, k], wts.a2[:, f], part[:, b, k], start=f == 0 and k == 0 and q == 0, stop=False,
                                         skip_group_check=True)
                if f == 0 and t.at_least(2):
                    pe.wait_ge(y_ready, GT * (t.n - 1))
                for j in range(GT):
                    rows = slice(j * P, (j + 1) * P)
                    for q, (x_, w_) in enumerate(SPLIT_PAIRS):
                        last = nc.tensor.matmul(ps_y[:, t.u, j], (h_hi, h_lo)[x_][:, b, 2, rows], wts.w2[:, w_, f],
                                                start=f == 0 and q == 0, stop=False, skip_group_check=True)
                last.then_inc(used, 1)

            def close(p):
                pe.wait_ge(z2_ready, p.n + 1)
                for j in range(GT):
                    rows = slice(j * P, (j + 1) * P)
                    for q, (x_, w_) in enumerate(SPLIT_PAIRS):
                        last = nc.tensor.matmul(ps_y[:, p.u, j], z2s[:, x_, rows], wts.b2[:, w_], start=False, stop=q == 2,
                                                skip_group_check=True)
                    last.then_inc(y_done, 1)

            def step(t):
                p = t.shift(-1)
                if isinstance(t.n, int) and t.n == 0:
                    base(t, 0)
                for f in range(FT):
                    if t.real:
                        if f + 1 < FT:
                            base(t, f + 1)
                        elif t.shift(1).real:
                            base(t.shift(1), 0)
                        moved(t, f)
                        if f > 0:
                            down(t, f - 1)
                        elif p.real:
                            down(p, FT - 1)
                    elif p.real and f == 0:
                        down(p, FT - 1)
                    if p.real and f == 2:
                        close(p)

            pipelined(pe, step=step, **STAGES)


def rope_table(T, D=32, base=10000.0):
    f32 = np.float32
    inv = (f32(1.0) / f32(base) ** (np.arange(0, D, 2, dtype=f32) / f32(D))).astype(f32)
    ang = np.outer(np.arange(T, dtype=f32), inv)
    cos, sin = np.cos(ang), np.sin(ang)
    return np.concatenate([cos, cos, -sin, sin], axis=1)


def mask_tables(T, block=64):
    before = np.zeros((32, T), np.float32)
    inside = np.zeros((32, T), np.float32)
    q = np.arange(T)
    for b in range(T // block):
        before[b] = q < block * b
        inside[b] = np.where(q // block == b, np.float32(-2.0**60), np.float32(0))
    inside[16:18] = 1.0
    return before, inside, np.ascontiguousarray(before[:16].T)


def build_program(nc, t, out):
    N, C = t["x"].shape
    F = t["w1"].shape[1]
    ER = t["a2"].shape[1]

    def scratch(name, *shape):
        return nc.dram_tensor(name, list(shape), F32, kind="Internal").ap()

    q_rows, k_rows, v_rows = (scratch(n, N, C) for n in ("q_rows", "k_rows", "v_rows"))
    ctx_rows, x1_rows = scratch("ctx_rows", N, C), scratch("x1_rows", N, C)
    xnT_cols = scratch("xnT_cols", P, 2, C // P, N)
    zm_cols = scratch("zm_cols", 2 * ER, 4, N)
    w_rows = scratch("w_rows", 2, N)

    project_phase(nc, t["x"], t["w_qkv"], t["rope"], q_rows, k_rows, v_rows)
    attention_phase(nc, q_rows, k_rows, v_rows, t["aux_q"], t["aux_k"], t["q_first_of_block"], ctx_rows)
    with Space(nc, "f_") as s:
        w_sum = s.sb("w_sum", [P, N // P])
        mix_phase(nc, ctx_rows, t["x"], t["w_o"], t["w_ra"], t["b_r"], t["iota8"],
                  x1_rows, xnT_cols, zm_cols, w_rows, w_sum)
        wts = ExpertWeights(s, C, F, ER)
        load_experts(nc, wts, t["w1"], t["w2"], t["a2"], t["b1_lora"], t["b2_lora"])
        expert_phase(nc, wts, xnT_cols, zm_cols, w_rows, w_sum, x1_rows, t["b1_cols"], t["b2"], out)


def kernel(L0_attn_x, L0_attn_w_q, L0_attn_w_k, L0_attn_w_v, L0_attn_w_o, L0_ffn_W_r, L0_ffn_b_r,
           L0_ffn_W1, L0_ffn_b1, L0_ffn_W2, L0_ffn_b2, L0_ffn_A1, L0_ffn_B1, L0_ffn_A2, L0_ffn_B2):
    import concourse.bacc as bacc
    from concourse.bass_utils import run_bass_kernel_spmd

    B, T, C = L0_attn_x.shape
    E, R, F = L0_ffn_A2.shape
    before, inside, q_first_of_block = mask_tables(T)
    inputs = {
        "x": L0_attn_x.reshape(B * T, C),
        "w_qkv": np.concatenate([L0_attn_w_q.T, L0_attn_w_k.T, L0_attn_w_v.T], axis=1),
        "rope": rope_table(T),
        "aux_q": before,
        "aux_k": inside,
        "q_first_of_block": q_first_of_block,
        "w_o": L0_attn_w_o.T,
        "w_ra": np.concatenate([L0_ffn_A1.reshape(E * R, C), L0_ffn_W_r], axis=0).T,
        "b_r": L0_ffn_b_r,
        "iota8": np.arange(-E, 0).astype(np.float32),
        "w1": L0_ffn_W1.T,
        "w2": L0_ffn_W2.T,
        "a2": L0_ffn_A2.reshape(E * R, F).T,
        "b1_lora": L0_ffn_B1.transpose(0, 2, 1).reshape(E * R, F),
        "b2_lora": L0_ffn_B2.transpose(0, 2, 1).reshape(E * R, C),
        "b1_cols": L0_ffn_b1.reshape(F // P, P).T,
        "b2": L0_ffn_b2,
    }
    inputs = {name: np.ascontiguousarray(a) for name, a in inputs.items()}
    nc = bacc.Bacc("TRN2", target_bir_lowering=False, num_devices=1)
    tensors = {name: nc.dram_tensor(name, list(a.shape), F32, kind="ExternalInput").ap() for name, a in inputs.items()}
    out = nc.dram_tensor("out", [B * T, C], F32, kind="ExternalOutput").ap()
    build_program(nc, tensors, out)
    result = run_bass_kernel_spmd(nc, [inputs], core_ids=[0])
    return result.results[0]["out"].reshape(B, T, C)
```

```python
from contextlib import ExitStack

import numpy as np

import concourse.bass as bass
from concourse import mybir

F32 = mybir.dt.float32
F32R = mybir.dt.float32r
BF16 = mybir.dt.bfloat16
F16 = mybir.dt.float16
ALU = mybir.AluOpType
ACT = mybir.ActivationFunctionType
AX_X = mybir.AxisListType.X

P = 128
EPS = 1e-5

SPLIT_PAIRS = ((0, 0), (1, 0), (0, 1))


class Space:

    def __init__(self, nc, prefix):
        self.nc, self.prefix, self.stack = nc, prefix, ExitStack()

    def __enter__(self):
        return self

    def __exit__(self, *a):
        return self.stack.__exit__(*a)

    def sb(self, name, shape, dt=F32):
        return self.stack.enter_context(self.nc.sbuf_tensor(self.prefix + name, shape, dt))

    def ps(self, name, shape, dt=F32):
        return self.stack.enter_context(self.nc.psum_tensor(self.prefix + name, shape, dt))

    def sem(self, name):
        return self.stack.enter_context(self.nc.semaphore(self.prefix + name))

    def sems(self, name, n):
        return [self.sem(f"{name}{i}") for i in range(n)]

    def block(self):
        return self.stack.enter_context(self.nc.Block())


def wait_apart(eng, sem, value, waited):
    eng.wait_ge(sem, value)
    eng.sem_inc(waited, 1)


def make_norm_constants(nc, pool, norm_consts, made):
    for k, value in enumerate((-0.5, EPS, -1.0)):
        nc.gpsimd.memset(norm_consts[:, k:k + 1], value).then_inc(made, 1)
    pool.wait_ge(made, 3)


def layer_norm_coefficients(nc, pool, norm_consts, mean_var, coef, stats_ready, eps_added, rstd_ready, shift_ready, count):
    neg_half, eps, neg_one = (norm_consts[:, k:k + 1] for k in range(3))
    var_eps, neg_mean, rstd, shift = (coef[:, k:k + 1] for k in range(4))
    pool.wait_ge(stats_ready, count)
    nc.gpsimd.tensor_tensor(var_eps, mean_var[:, 1:2], eps, ALU.add)
    nc.gpsimd.tensor_tensor(neg_mean, mean_var[:, 0:1], neg_one, ALU.mult).then_inc(eps_added, 1)
    pool.wait_ge(eps_added, count)
    nc.gpsimd.tensor_tensor(rstd, var_eps, neg_half, ALU.pow).then_inc(rstd_ready, 1)
    pool.wait_ge(rstd_ready, count)
    nc.gpsimd.tensor_tensor(shift, neg_mean, rstd, ALU.mult).then_inc(shift_ready, 1)


def make_identity(nc, eng, identity, made):
    nc.gpsimd.memset(identity[:], 0.0).then_inc(made, 1)
    eng.wait_ge(made, 1)
    nc.gpsimd.affine_select(out=identity[:], in_=identity[:], compare_op=ALU.not_equal, fill=1.0,
                            base=0, pattern=[[-1, P]], channel_multiplier=1).then_inc(made, 1)


def project_phase(nc, x, w_qkv, rope, q_rows, k_rows, v_rows):
    N, C = x.shape
    T = rope.shape[0]
    NT, CT = N // P, C // P
    TT = T // P
    H, D = C // 32, 32
    with Space(nc, "a_") as s:
        identity = s.sb("identity", [P, P])
        w_raw = s.sb("w_raw", [P, CT, 3 * C])
        w = s.sb("w", [P, 2, CT, 3 * C], F32R)
        rope_sb = s.sb("rope_sb", [P, TT, 2, D])
        x_sb = s.sb("x_sb", [P, 2, C])
        stats = s.sb("stats", [P, 2, 6])
        mean_var = s.sb("mean_var", [P, 2, 2])
        norm_consts = s.sb("norm_consts", [P, 3])
        coef = s.sb("coef", [P, 2, 4])
        xn = s.sb("xn", [P, 2, C])
        xnT = s.sb("xnT", [P, 2, 2, CT, P], F32R)
        by_cos = s.sb("by_cos", [P, 2, 2, C])
        by_sin = s.sb("by_sin", [P, 2, 2, C])
        v_sb = s.sb("v_sb", [P, 2, C])
        ps_xT = s.ps("ps_xT", [P, 2, CT, P])
        ps_qkv = s.ps("ps_qkv", [P, 2, 3, C])

        id_made = s.sem("id_made")
        norm_consts_made = s.sem("norm_consts_made")
        w_loaded = s.sems("w_loaded", CT)
        rope_loaded = s.sem("rope_loaded")
        w_hi_ready, w_lo_ready = s.sem("w_hi_ready"), s.sem("w_lo_ready")
        x_loaded = s.sems("x_loaded", 2)
        bn_ready, stats_ready = s.sem("bn_ready"), s.sem("stats_ready")
        eps_added, rstd_ready, shift_ready = s.sem("eps_added"), s.sem("rstd_ready"), s.sem("shift_ready")
        xn_ready = s.sem("xn_ready")
        xT_in_psum = s.sem("xT_in_psum")
        xT_hi_ready, xT_lo_ready = s.sem("xT_hi_ready"), s.sem("xT_lo_ready")
        projected = s.sem("projected")
        rope_parts = s.sem("rope_parts")
        rotated = s.sem("rotated")
        v_ready = s.sem("v_ready")
        qk_free, v_free = s.sems("qk_free", 2), s.sems("v_free", 2)
        waited = s.sem("waited")
        block = s.block()

        @block.sync
        def _(sp):
            wr = w_qkv.rearrange("(c p) o -> p c o", p=P)

            def load(m, u):
                sp.dma_start(x_sb[:, u], x[bass.ds(m * P, P), :]).then_inc(x_loaded[u], 16)

            load(0, 0)
            load(1, 1)
            for c in range(CT):
                sp.dma_start(w_raw[:, c], wr[:, c]).then_inc(w_loaded[c], 16)
            sp.dma_start(rope_sb[:], rope.rearrange("(t p) r -> p t r", p=P)
                         .rearrange("p t (a d) -> p t a d", a=2)).then_inc(rope_loaded, 16)
            for u in range(2):
                sp.sem_inc(qk_free[u], 32)
                sp.sem_inc(v_free[u], 16)

            def tile(n, u, it, last):
                if not last:
                    sp.wait_ge(xn_ready, n + 1)
                    load(n + 2, u)
                sp.wait_ge(rotated, 2 * n + 1)
                sp.dma_start(q_rows[bass.ds(n * P, P), :], by_cos[:, u, 0]).then_inc(qk_free[u], 16)
                sp.wait_ge(rotated, 2 * n + 2)
                sp.dma_start(k_rows[bass.ds(n * P, P), :], by_cos[:, u, 1]).then_inc(qk_free[u], 16)
                sp.wait_ge(v_ready, n + 1)
                sp.dma_start(v_rows[bass.ds(n * P, P), :], v_sb[:, u]).then_inc(v_free[u], 16)

            with sp.Fori(0, NT // 2 - 1) as it:
                for u in range(2):
                    tile(2 * it + u, u, it, False)
            for u in range(2):
                tile(NT - 2 + u, u, NT // 2 - 1, True)
            for u in range(2):
                sp.wait_ge(qk_free[u], 32 * (NT // 2 + 1))
                sp.wait_ge(v_free[u], 16 * (NT // 2 + 1))

        @block.gpsimd
        def _(pool):
            make_identity(nc, pool, identity, id_made)
            make_norm_constants(nc, pool, norm_consts, norm_consts_made)

            def coefficients(m, u):
                layer_norm_coefficients(nc, pool, norm_consts, mean_var[:, u], coef[:, u],
                                        stats_ready, eps_added, rstd_ready, shift_ready, m + 1)

            coefficients(0, 0)
            coefficients(1, 1)

            def tile(n, u, last):
                if not last:
                    coefficients(n + 2, u)
                for j in range(2):
                    pool.wait_ge(rope_parts, 2 * n + j + 1)
                    nc.gpsimd.tensor_tensor(by_cos[:, u, j], by_cos[:, u, j], by_sin[:, u, j], ALU.add).then_inc(rotated, 1)

            with pool.Fori(0, NT // 2 - 1) as it:
                for u in range(2):
                    tile(2 * it + u, u, False)
            for u in range(2):
                tile(NT - 2 + u, u, True)

        @block.scalar
        def _(act):
            def normalise(m, u):
                act.wait_ge(shift_ready, m + 1)
                nc.scalar.activation(xn[:, u], x_sb[:, u], ACT.Identity, bias=coef[:, u, 3:4],
                                     scale=coef[:, u, 2:3]).then_inc(xn_ready, 1)

            def take_hi(m, u, it):
                act.wait_ge(xT_in_psum, m + 1)
                if it is not None:
                    act.wait_ge(projected, 3 * m - 3)
                nc.scalar.activation(xnT[:, u, 0], ps_xT[:, u], ACT.Copy).then_inc(xT_hi_ready, 1)

            normalise(0, 0)
            for c in range(CT):
                act.wait_ge(w_loaded[c], 16)
                nc.scalar.activation(w[:, 0, c], w_raw[:, c], ACT.Copy).then_inc(w_hi_ready, 1)
            take_hi(0, 0, None)
            normalise(1, 1)

            def tile(n, u, it, last):
                if not (last and u == 1):
                    if isinstance(n, int) and n == 0:
                        take_hi(1, 1, None)
                    else:
                        take_hi(n + 1, 1 - u, it)
                if not last:
                    normalise(n + 2, u)
                act.wait_ge(projected, 3 * n + 3)
                act.wait_ge(v_free[u], 16 * (it + 1))
                nc.scalar.activation(v_sb[:, u], ps_qkv[:, u, 2], ACT.Copy).then_inc(v_ready, 1)

            for u in range(2):
                tile(u, u, 0, False)
            with act.Fori(1, NT // 2 - 1) as it:
                for u in range(2):
                    tile(2 * it + u, u, it, False)
            for u in range(2):
                tile(NT - 2 + u, u, NT // 2 - 1, True)

        @block.vector
        def _(dve):
            def statistics(m, u, it):
                dve.wait_ge(x_loaded[u], 16 * (it + 1))
                nc.vector.bn_stats(stats[:, u], x_sb[:, u]).then_inc(bn_ready, 1)
                wait_apart(dve, bn_ready, m + 1, waited)
                nc.vector.bn_aggr(mean_var[:, u], stats[:, u]).then_inc(stats_ready, 1)

            def take_lo(m, u):
                dve.wait_ge(xT_hi_ready, m + 1)
                nc.vector.tensor_tensor(xnT[:, u, 1], ps_xT[:, u], xnT[:, u, 0].bitcast(F32), ALU.subtract).then_inc(xT_lo_ready, 1)

            statistics(0, 0, 0)
            statistics(1, 1, 0)
            for c in range(CT):
                dve.wait_ge(w_hi_ready, c + 1)
                nc.vector.tensor_tensor(w[:, 1, c], w_raw[:, c], w[:, 0, c].bitcast(F32), ALU.subtract).then_inc(w_lo_ready, 1)
            take_lo(0, 0)
            dve.wait_ge(rope_loaded, 16)

            def rope_tile(n, u, it, t):
                cos = rope_sb[:, t, 0].unsqueeze(1).broadcast_to([P, H, D])
                for j in range(2):
                    src = ps_qkv[:, u, j].rearrange("p (h d) -> p h d", d=D)
                    dve.wait_ge(projected, 3 * n + j + 1)
                    dve.wait_ge(qk_free[u], 32 * (it + 1))
                    nc.vector.tensor_tensor(by_cos[:, u, j].rearrange("p (h d) -> p h d", d=D), src, cos, ALU.mult)
                    dst = by_sin[:, u, j].rearrange("p (h d) -> p h d", d=D)
                    half = D // 2
                    for a, b in ((0, half), (half, 0)):
                        sin = rope_sb[:, t, 1, a:a + half].unsqueeze(1).broadcast_to([P, H, half])
                        last = nc.vector.tensor_tensor(dst[:, :, a:a + half], src[:, :, b:b + half], sin, ALU.mult)
                    last.then_inc(rope_parts, 1)

            def tile(n, u, it, t, last):
                if not (last and u == 1):
                    take_lo(n + 1, 1 - u)
                if not last:
                    statistics(n + 2, u, it + 1)
                rope_tile(n, u, it, t)

            reps = NT // TT
            with dve.Fori(0, reps - 1) as b:
                for t in range(TT):
                    tile(b * TT + t, t % 2, b * (TT // 2) + t // 2, t, False)
            for t in range(TT):
                n = (reps - 1) * TT + t
                tile(n, t % 2, n // 2, t, t >= TT - 2)

        @block.tensor
        def _(pe):
            def transpose(m, u, it):
                pe.wait_ge(xn_ready, m + 1)
                if it is not None:
                    pe.wait_ge(xT_lo_ready, m - 1)
                for c in range(CT):
                    last = nc.tensor.transpose(ps_xT[:, u, c], xn[:, u, c * P:(c + 1) * P], identity[:])
                last.then_inc(xT_in_psum, 1)

            pe.wait_ge(id_made, 2)
            transpose(0, 0, None)
            pe.wait_ge(w_lo_ready, CT)

            def project(n, u, it):
                pe.wait_ge(xT_lo_ready, n + 1)
                for j in range(3):
                    if it is not None:
                        if j < 2:
                            pe.wait_ge(rope_parts, 2 * n - 3 + j)
                        else:
                            pe.wait_ge(v_ready, n - 1)
                    k = 0
                    for c in range(CT):
                        for a, b in SPLIT_PAIRS:
                            last = nc.tensor.matmul(ps_qkv[:, u, j], xnT[:, u, a, c], w[:, b, c, j * C:(j + 1) * C],
                                                    start=k == 0, stop=k == 3 * CT - 1)
                            k += 1
                    last.then_inc(projected, 1)

            for n in range(2):
                transpose(n + 1, 1 - n, None if n == 0 else 0)
                project(n, n, None)
            with pe.Fori(1, NT // 2 - 1) as it:
                for u in range(2):
                    transpose(2 * it + u + 1, 1 - u, it)
                    project(2 * it + u, u, it)
            transpose(NT - 1, 1, 0)
            project(NT - 2, 0, 0)
            project(NT - 1, 1, 0)


def attention_phase(nc, q_rows, k_rows, v_rows, aux_q, aux_k, q_first_of_block, ctx_rows):
    N, C = q_rows.shape
    T = aux_q.shape[1]
    B = N // T
    HI = 4
    HG = C // (HI * 32)
    ITEMS = B * HG
    D = 32
    W = HI * D
    TT = T // P
    G = 512
    GT = G // P
    NG = T // G
    AUX = 96
    MROW = AUX + 16
    VW = 1 + 3 * D
    SCALE = 1.0 / float(np.sqrt(D))

    first = []
    for t in range(TT):
        n = (t + 1) * P
        for part in range((n + G - 1) // G):
            first.append((t, part * G, min(G, n - part * G), part))
    second = [(g, kt, max(0, kt - GT * g)) for g in range(NG) for kt in range(GT * (g + 1))]
    NF, NS = len(first), len(second)
    assert NF == NS == 12 and NG == 2
    FG0 = sum(1 for f in first if f[0] < GT)
    POOL_LO = (1, 3, 5, 7, 9, 11)
    DVE_LO = tuple(j for j in range(NS) if j not in POOL_LO)
    SB = 3
    MISC = (("shift1", 1), ("stack", 3), ("stack", 5), ("stack", 6), ("stack", 8), ("shift0", 9))
    NM = len(MISC)
    LAG = 3
    RP = 6
    V_PARTS = {1: (0,), 3: (1,), 5: (2,), 7: (3,), 9: (4,)}
    PV0, SF0, CF0 = RP, SB, NG

    with Space(nc, "b_") as s:
        identity = s.sb("identity", [P, P])
        identity_r = s.sb("identity_r", [P, P], F32R)
        aux_raw = s.sb("aux_raw", [32, 2, T])
        qf_raw = s.sb("qf_raw", [P, TT, 16])
        q_in = s.sb("q_in", [P, 2, TT, W])
        k_in = s.sb("k_in", [P, 2, TT, W])
        v_in = s.sb("v_in", [P, 2, TT, W])
        q96 = s.sb("q96", [P, 2, TT, HI, 3 * D], F32R)
        k96 = s.sb("k96", [P, 2, TT, HI, 3 * D], F32R)
        v_rest = s.sb("v_rest", [P, 2, W])
        v3 = s.sb("v3", [P, 2, TT, HI, VW], BF16)
        qT = s.sb("qT", [P, 2, HI, T], F32R)
        kT = s.sb("kT", [P, 2, HI, T], F32R)
        shiftc = s.sb("shiftc", [P, TT, P], F32R)
        pmax = s.sb("pmax", [P, TT, 2])
        negmax = s.sb("negmax", [P, TT])
        prob = s.sb("prob", [P, RP, G])
        p_hi = s.sb("p_hi", [P, RP, G], F16)
        p_lo = s.sb("p_lo", [P, RP, G], F16)
        parts = s.sb("parts", [P, 2, GT, D])
        recip = s.sb("recip", [P, 2, GT])
        ctx_sb = s.sb("ctx_sb", [P, 2, TT, W])
        ps_first = s.ps("ps_first", [P, 2, G])
        ps_second = s.ps("ps_second", [P, SB, G])
        ps_misc = s.ps("ps_misc", [P, G])
        ps_ctx = s.ps("ps_ctx", [P, 2, G])

        id_made, id_r_made = s.sem("id_made"), s.sem("id_r_made")
        aux_loaded = s.sem("aux_loaded")
        zeroed, aux_ready, aux_spread = (s.sem(x) for x in ("zeroed", "aux_ready", "aux_spread"))
        q_loaded, k_loaded, v_loaded = s.sems("q_loaded", 2), s.sems("k_loaded", 2), s.sems("v_loaded", 2)
        hi_made, qk_split = s.sem("hi_made"), s.sem("qk_split")
        v_stage, v_split = s.sem("v_stage"), s.sem("v_split")
        first_done, first_read = s.sem("first_done"), s.sem("first_read")
        negmax_made, shift_hi_made, shift_written = s.sem("negmax_made"), s.sem("shift_hi_made"), s.sem("shift_written")
        misc_full, misc_free = s.sem("misc_full"), s.sem("misc_free")
        second_done = s.sem("second_done")
        prob_ready, p_hi_ready = s.sem("prob_ready"), s.sem("p_hi_ready")
        lo_dve, lo_pool = s.sem("lo_dve"), s.sem("lo_pool")
        pv_done = s.sem("pv_done")
        parts_ready, ctx_ready = s.sem("parts_ready"), s.sem("ctx_ready")
        ctx_stored = s.sems("ctx_stored", 2)
        waited = s.sem("waited")
        block = s.block()

        def pairs(eng, step):
            with eng.Fori(0, ITEMS // 2 - 1) as it:
                for u in range(2):
                    for h in range(HI):
                        step(2 * it + u, u, h, it, False)
            for u in range(2):
                for h in range(HI):
                    step(ITEMS - 2 + u, u, h, ITEMS // 2 - 1, True)

        def splits_item(u, last):
            return not last

        def stacks_item(u, last):
            return not (last and u == 1)

        def has_next_step(u, h, last):
            return not (last and u == 1 and h == HI - 1)

        def step_of(i, h):
            return HI * i + h

        def next_step(i, u, h, it, last):
            return (i, u, h + 1, it, last) if h < HI - 1 else (i + 1, 1 - u, 0, it + u, last)

        opening_stacks = [(h, k) for h in range(HI) for k in (0, 2, 1, 3)]

        def opening_bank(m):
            return ps_misc[:] if m % (SB + 1) == SB else ps_second[:, m % (SB + 1)]

        @block.sync
        def _(sp):
            sp.dma_start(aux_raw[:, 0], aux_q).then_inc(aux_loaded, 16)
            sp.dma_start(aux_raw[:, 1], aux_k).then_inc(aux_loaded, 16)
            sp.dma_start(qf_raw[:], q_first_of_block.rearrange("(t p) b -> p t b", p=P)).then_inc(aux_loaded, 16)

            QK = ((q_in, q_rows, q_loaded), (k_in, k_rows, k_loaded))
            V = ((v_in, v_rows, v_loaded),)

            def load(which, i, u):
                row, col = (i // HG) * T, (i % HG) * W
                for dst, src, sem in which:
                    sp.dma_start(dst[:, u], src[bass.ds(row, T), bass.ds(col, W)].rearrange("(t p) w -> p t w", p=P)).then_inc(sem[u], 16)

            for i in range(2):
                load(QK, i, i)
                load(V, i, i)
            sp.wait_ge(aux_ready, 1)
            for rows in (qT, kT):
                head0 = rows[AUX:P, 0, 0].bitcast(F32).unsqueeze(1)
                sp.dma_start(rows[AUX:P, 0, 1:HI].bitcast(F32), head0.broadcast_to([P - AUX, HI - 1, T])).then_inc(aux_spread, 16)
                sp.dma_start(rows[AUX:P, 1].bitcast(F32), head0.broadcast_to([P - AUX, HI, T])).then_inc(aux_spread, 16)
            for u in range(2):
                sp.sem_inc(ctx_stored[u], 16)
            sp.wait_ge(qk_split, HI)
            load(QK, 2, 0)
            sp.wait_ge(v_split, HI)
            load(V, 2, 0)
            sp.wait_ge(qk_split, 2 * HI)
            load(QK, 3, 1)

            def store(i, u):
                row, col = (i // HG) * T, (i % HG) * W
                sp.dma_start(ctx_rows[bass.ds(row, T), bass.ds(col, W)].rearrange("(t p) w -> p t w", p=P), ctx_sb[:, u]).then_inc(ctx_stored[u], 16)

            with sp.Fori(0, ITEMS // 2 - 2) as it:
                for u in range(2):
                    sp.wait_ge(qk_split, HI * (2 * it + u + 3))
                    load(QK, 2 * it + u + 4, u)
                    sp.wait_ge(v_split, HI * (2 * it + u + 2))
                    load(V, 2 * it + u + 3, 1 - u)
                    sp.wait_ge(ctx_ready, CF0 + NG * HI * (2 * it + u + 1))
                    store(2 * it + u, u)
            sp.wait_ge(v_split, HI * (ITEMS - 2))
            load(V, ITEMS - 1, 1)
            for i in range(ITEMS - 4, ITEMS):
                sp.wait_ge(ctx_ready, CF0 + NG * HI * (i + 1))
                store(i, i % 2)
            for u in range(2):
                sp.wait_ge(ctx_stored[u], 16 * (ITEMS // 2 + 1))

        @block.gpsimd
        def _(pool):
            make_identity(nc, pool, identity, id_made)
            nc.gpsimd.memset(v3[:, :, :, :, 0:1], 1.0)

            def split_v(i, u, quarter, k):
                tiles = slice(2 * quarter, 2 * quarter + 2)
                vin = v_in[:, u, tiles].rearrange("p t (h d) -> p (t h) d", d=D)
                rest = v_rest[:].rearrange("p t (h d) -> p (t h) d", d=D)
                rows = v3[:, u, tiles].rearrange("p t h w -> p (t h) w")
                part = [rows[:, :, 1 + D * n:1 + D * (n + 1)] for n in range(3)]
                if k > 0:
                    wait_apart(pool, v_stage, 4 * (HI * i + quarter) + k, waited)
                if k == 0:
                    nc.gpsimd.tensor_copy(part[0], vin).then_inc(v_stage, 1)
                elif k == 1:
                    nc.gpsimd.tensor_tensor(rest, vin, part[0], ALU.subtract).then_inc(v_stage, 1)
                elif k == 2:
                    nc.gpsimd.tensor_copy(part[1], rest).then_inc(v_stage, 1)
                elif k == 3:
                    nc.gpsimd.tensor_tensor(rest, rest, part[1], ALU.subtract).then_inc(v_stage, 1)
                else:
                    nc.gpsimd.tensor_copy(part[2], rest).then_inc(v_split, 1)

            pool.wait_ge(v_loaded[0], 16)
            for c in range(HI):
                for k in range(5):
                    if c > 0 and k == 1:
                        pool.wait_ge(v_split, c)
                    split_v(0, 0, c, k)

            def step(i, u, h, it, last):
                n = step_of(i, h)
                for j in POOL_LO:
                    w = G - P * second[j][2]
                    pool.wait_ge(p_hi_ready, SF0 + NS * n + j + 1)
                    nc.gpsimd.tensor_tensor(p_lo[:, j % RP, :w], prob[:, j % RP, :w], p_hi[:, j % RP, :w], ALU.subtract).then_inc(lo_pool, 1)
                    if not stacks_item(u, last):
                        continue
                    for k in V_PARTS.get(j, ()):
                        if h == 0 and k == 0:
                            pool.wait_ge(v_loaded[1 - u], 16 * (it + u + 1))
                            wait_apart(pool, pv_done, PV0 + NS * n, waited)
                        if k == 1:
                            pool.wait_ge(v_split, HI * (i + 1) + h)
                        split_v(i + 1, 1 - u, h, k)

            pairs(pool, step)

        @block.scalar
        def _(act):
            act.sem_inc(p_hi_ready, SF0)
            act.wait_ge(id_made, 2)
            nc.scalar.activation(identity_r[:], identity[:], ACT.Copy).then_inc(id_r_made, 1)
            act.wait_ge(aux_loaded, 48)
            nc.scalar.activation(qT[AUX:P, 0, 0], aux_raw[:, 0], ACT.Copy)
            nc.scalar.activation(kT[AUX:P, 0, 0], aux_raw[:, 1], ACT.Copy).then_inc(aux_ready, 1)

            def stack_to(k, src, u, h):
                dst = (qT, kT)[k // 2]
                return nc.scalar.activation(dst[0:AUX, u, h, (k % 2) * G:(k % 2 + 1) * G], src, ACT.Copy)

            for m, (h, k) in enumerate(opening_stacks):
                act.wait_ge(misc_full, m + 1)
                stack_to(k, opening_bank(m)[0:AUX], 0, h).then_inc(misc_free, 1)
            act.wait_ge(aux_spread, 64)
            act.wait_ge(misc_full, 4 * HI + 1)
            nc.scalar.activation(qT[AUX:P, 0, 0, 0:G], ps_misc[AUX:P], ACT.Copy).then_inc(misc_free, 1)

            def step(i, u, h, it, last):
                n = step_of(i, h)
                stacks = 0
                misc = {}
                for k, (what, j) in enumerate(MISC):
                    misc[j] = (k, what)
                for j, (g, kt, t0) in enumerate(second):
                    w = G - P * t0
                    act.wait_ge(second_done, NS * n + j + 1)
                    act.wait_ge(pv_done, PV0 + NS * n + j + 1 - RP)
                    nc.scalar.activation(prob[:, j % RP, :w], ps_second[:, j % SB, :w], ACT.Exp, scale=SCALE).then_inc(prob_ready, 1)
                    nc.scalar.activation(p_hi[:, j % RP, :w], ps_second[:, j % SB, :w], ACT.Exp, scale=SCALE).then_inc(p_hi_ready, 1)
                    if j in misc:
                        k, what = misc[j]
                        if what == "stack" and stacks_item(u, last):
                            act.wait_ge(misc_full, misc_base(n) + k + 1)
                            stack_to(stacks, ps_misc[0:AUX], 1 - u, h).then_inc(misc_free, 1)
                        elif what == "shift1":
                            act.wait_ge(misc_full, misc_at(i, u, h, last, k) + 1)
                            nc.scalar.activation(qT[AUX:P, u, h, G:2 * G], ps_misc[AUX:P], ACT.Copy).then_inc(misc_free, 1)
                        elif what == "shift0" and has_next_step(u, h, last):
                            u2, h2 = (u, h + 1) if h < HI - 1 else (1 - u, 0)
                            act.wait_ge(misc_full, misc_at(i, u, h, last, k) + 1)
                            nc.scalar.activation(qT[AUX:P, u2, h2, 0:G], ps_misc[AUX:P], ACT.Copy).then_inc(misc_free, 1)
                        stacks += what == "stack"

            def misc_base(n):
                return 4 * HI + 1 + NM * n

            def misc_at(i, u, h, last, k):
                return misc_base(step_of(i, h)) + k if stacks_item(u, last) else misc_base(step_of(ITEMS - 1, 0)) + 2 * h + (k > 0)

            pairs(act, step)

        @block.vector
        def _(dve):
            dve.sem_inc(ctx_ready, CF0)
            dve.wait_ge(aux_loaded, 48)
            nc.vector.memset(shiftc[:].bitcast(mybir.dt.uint32), 0).then_inc(zeroed, 1)
            nc.vector.memset(pmax[:], 3e38).then_inc(zeroed, 1)
            dve.wait_ge(zeroed, 2)
            nc.vector.tensor_copy(shiftc[:, :, AUX:MROW], qf_raw[:])

            def split_qk(i, u, quarter, m):
                tiles = slice(2 * quarter, 2 * quarter + 2)
                for src, dst, twice in ((q_in, q96, (0, 1)), (k_in, k96, (0, 2))):
                    raw = src[:, u, tiles].rearrange("p t (h d) -> p (t h) d", d=D)
                    out = dst[:, u, tiles].rearrange("p t h (a d) -> p (t h) a d", d=D)
                    both = out[:, :, twice[0]:twice[1] + 1:twice[1] - twice[0], :]
                    nc.vector.tensor_copy(both, raw.unsqueeze(2).broadcast_to([P, 2 * HI, 2, D])).then_inc(hi_made, 1)
                dve.wait_ge(hi_made, 2 * m + 2)
                for src, dst, lo in ((q_in, q96, 2), (k_in, k96, 1)):
                    raw = src[:, u, tiles].rearrange("p t (h d) -> p (t h) d", d=D)
                    out = dst[:, u, tiles].rearrange("p t h (a d) -> p (t h) a d", d=D)
                    last = nc.vector.tensor_tensor(out[:, :, lo], raw, out[:, :, 0].bitcast(F32), ALU.subtract)
                last.then_inc(qk_split, 1)

            def split_whole(i):
                dve.wait_ge(q_loaded[i], 16)
                dve.wait_ge(k_loaded[i], 16)
                for c in range(HI):
                    split_qk(i, i, c, HI * i + c)

            split_whole(0)

            def reduce(m, n, j):
                t, k0, w, part = first[j]
                dve.wait_ge(first_done, m + 1)
                out = negmax[:, t:t + 1] if t < GT else pmax[:, t, part:part + 1]
                nc.vector.tensor_reduce(out, ps_first[:, j % 2, :w], AX_X, ALU.max, negate=True).then_inc(first_read, 1)

            def write_shift(n, g):
                tiles = slice(GT * g, GT * (g + 1))
                if g == 0:
                    dve.wait_ge(first_read, NF * n + FG0)
                else:
                    dve.wait_ge(first_read, NF * n + NF)
                    nc.vector.tensor_reduce(negmax[:, tiles], pmax[:, tiles], AX_X, ALU.min).then_inc(negmax_made, 1)
                    dve.wait_ge(negmax_made, n + 1)
                nc.vector.tensor_copy(shiftc[:, tiles, MROW], negmax[:, tiles]).then_inc(shift_hi_made, 1)
                dve.wait_ge(shift_hi_made, 2 * n + g + 1)
                nc.vector.tensor_tensor(shiftc[:, tiles, MROW + 1], negmax[:, tiles], shiftc[:, tiles, MROW].bitcast(F32),
                                        ALU.subtract).then_inc(shift_written, 1)

            for j in range(NF):
                reduce(j, 0, j)
                if j == FG0 - 1:
                    write_shift(0, 0)
            write_shift(0, 1)
            split_whole(1)

            def finish(i, u, h, g, n, it):
                m = NG * n + g
                dve.wait_ge(pv_done, PV0 + NS * n + (GT if g == 0 else NS))
                acc = ps_ctx[:, g, 0:GT * VW].rearrange("p (t w) -> p t w", w=VW)
                nc.vector.tensor_reduce(parts[:, g], acc[:, :, 1:VW].rearrange("p t (a d) -> p t d a", d=D), AX_X, ALU.add)
                nc.vector.reciprocal(recip[:, g], acc[:, :, 0]).then_inc(parts_ready, 1)
                dve.wait_ge(parts_ready, m + 1)
                if h == 0 and g == 0:
                    dve.wait_ge(ctx_stored[u], 16 * (it + 1))
                nc.vector.tensor_tensor(ctx_sb[:, u, GT * g:GT * (g + 1), h * D:(h + 1) * D], parts[:, g],
                                        recip[:, g].unsqueeze(2).broadcast_to([P, GT, D]), ALU.mult).then_inc(ctx_ready, 1)

            def lo_part(n, j):
                if j in DVE_LO:
                    w = G - P * second[j][2]
                    dve.wait_ge(p_hi_ready, SF0 + NS * n + j + 1)
                    nc.vector.tensor_tensor(p_lo[:, j % RP, :w], prob[:, j % RP, :w], p_hi[:, j % RP, :w], ALU.subtract).then_inc(lo_dve, 1)

            def chunk(i, u, h, it, last, j):
                n = step_of(i, h)
                if has_next_step(u, h, last):
                    reduce(NF * (n + 1) + j, n + 1, j)
                    if j == FG0 + 1:
                        write_shift(n + 1, 0)
                    if j == NF - 1:
                        write_shift(n + 1, 1)
                if j > 0:
                    lo_part(n, j - 1)
                if j == GT + LAG + 1:
                    finish(i, u, h, 0, n, it)
                if j == 9 and splits_item(u, last):
                    if h == 0:
                        dve.wait_ge(q_loaded[u], 16 * (it + 2))
                        dve.wait_ge(k_loaded[u], 16 * (it + 2))
                    split_qk(i + 2, u, h, HI * (i + 2) + h)

            AHEAD = LAG + 1
            for j in range(AHEAD):
                chunk(0, 0, 0, 0, False, j)

            def step(i, u, h, it, last):
                n = step_of(i, h)
                for j in range(AHEAD, NS):
                    chunk(i, u, h, it, last, j)
                if not has_next_step(u, h, last):
                    lo_part(n, NS - 1)
                else:
                    for j in range(AHEAD):
                        chunk(*next_step(i, u, h, it, last), j)
                        if j == 0:
                            lo_part(n, NS - 1)
                finish(i, u, h, 1, n, it)

            pairs(dve, step)

        @block.tensor
        def _(pe):
            def stack(k, u, h, bank):
                src = (q96, k96)[k // 2]
                for t in range(GT):
                    last = nc.tensor.matmul(bank[0:AUX, t * P:(t + 1) * P], src[:, u, (k % 2) * GT + t, h],
                                            identity_r[:], start=True, stop=True)
                last.then_inc(misc_full, 1)

            def shift(g):
                for t in range(GT):
                    last = nc.tensor.matmul(ps_misc[:, t * P:(t + 1) * P], shiftc[:, GT * g + t],
                                            identity_r[:], start=True, stop=True)
                last.then_inc(misc_full, 1)

            def first_pass(u, h, j):
                t, k0, w, part = first[j]
                nc.tensor.matmul(ps_first[:, j % 2, :w], qT[0:MROW, u, h, t * P:(t + 1) * P],
                                 kT[0:MROW, u, h, k0:k0 + w], start=True, stop=True).then_inc(first_done, 1)

            pe.sem_inc(pv_done, PV0)
            pe.wait_ge(id_r_made, 1)
            pe.wait_ge(aux_ready, 1)
            for m, (h, k) in enumerate(opening_stacks):
                if h == 0:
                    pe.wait_ge(qk_split, HI // 2 * (1 + k % 2))
                if m > SB:
                    pe.wait_ge(misc_free, m - SB)
                stack(k, 0, h, opening_bank(m))
                j = m - 4
                if j >= 0:
                    if j == 0:
                        pe.wait_ge(misc_free, 4)
                    if j >= 2:
                        pe.wait_ge(first_read, j - 1)
                    first_pass(0, 0, j)
            pe.wait_ge(aux_spread, 64)
            pe.wait_ge(shift_written, 1)
            pe.wait_ge(misc_free, 4 * HI)
            shift(0)

            def misc_at(i, u, h, last, k):
                base = 4 * HI + 1 + NM * step_of(i, h)
                return base + k if stacks_item(u, last) else 4 * HI + 1 + NM * step_of(ITEMS - 1, 0) + 2 * h + (k > 0)

            def with_v(n, u, h, j):
                g, kt, t0 = second[j]
                if j in DVE_LO:
                    pe.wait_ge(lo_dve, len(DVE_LO) * n + DVE_LO.index(j) + 1)
                else:
                    pe.wait_ge(lo_pool, len(POOL_LO) * n + POOL_LO.index(j) + 1)
                opening = kt == 0
                if opening:
                    pe.wait_ge(ctx_ready, CF0 + NG * n + g - 1)
                for t in range(t0, GT):
                    cols = slice((t - t0) * P, (t - t0 + 1) * P)
                    nc.tensor.matmul(ps_ctx[:, g, t * VW:(t + 1) * VW], p_hi[:, j % RP, cols], v3[:, u, kt, h],
                                     start=opening and t == 0, stop=False, skip_group_check=True)
                    last = nc.tensor.matmul(ps_ctx[:, g, t * VW:t * VW + 1 + 2 * D], p_lo[:, j % RP, cols],
                                            v3[:, u, kt, h, 0:1 + 2 * D], start=False, stop=False, skip_group_check=True)
                last.then_inc(pv_done, 1)

            def chunk(i, u, h, it, last, j):
                n = step_of(i, h)
                nxt = has_next_step(u, h, last)
                u2, h2 = (u, h + 1) if h < HI - 1 else (1 - u, 0)
                misc = {at: (k, what) for k, (what, at) in enumerate(MISC)}
                g, kt, t0 = second[j]
                w = G - P * t0
                if j == 0:
                    pe.wait_ge(misc_free, misc_at(i, u, h, last, 0))
                if kt == 0 and g == 1:
                    pe.wait_ge(misc_free, misc_at(i, u, h, last, 0) + 1)
                pe.wait_ge(p_hi_ready, NS * n + j + 1)
                nc.tensor.matmul(ps_second[:, j % SB, :w], kT[:, u, h, kt * P:(kt + 1) * P],
                                 qT[:, u, h, g * G + t0 * P:(g + 1) * G], start=True, stop=True).then_inc(second_done, 1)
                if nxt:
                    if j == 0 and h2 == 0:
                        pe.wait_ge(misc_free, misc_at(i, u, h, last, 0) - 1)
                    pe.wait_ge(first_read, NF * (n + 1) + j - 1)
                    first_pass(u2, h2, j)
                if j not in misc:
                    return
                k, what = misc[j]
                if what == "stack" and stacks_item(u, last):
                    if h == 0 and k == 1:
                        pe.wait_ge(qk_split, HI * (i + 2))
                    pe.wait_ge(misc_free, misc_at(i, u, h, last, k))
                    stack(k - 1, 1 - u, h, ps_misc)
                elif what == "shift1" or (what == "shift0" and nxt):
                    pe.wait_ge(shift_written, 2 * n + (2 if what == "shift1" else 3))
                    pe.wait_ge(misc_free, misc_at(i, u, h, last, k))
                    shift(int(what == "shift1"))

            for j in range(LAG):
                chunk(0, 0, 0, 0, False, j)

            def step(i, u, h, it, last):
                n = step_of(i, h)
                if h == 0:
                    pe.wait_ge(v_split, HI * (i + 1))
                for j in range(LAG, NS):
                    chunk(i, u, h, it, last, j)
                    with_v(n, u, h, j - LAG)
                for j in range(LAG):
                    if has_next_step(u, h, last):
                        chunk(*next_step(i, u, h, it, last), j)
                    with_v(n, u, h, NS - LAG + j)

            pairs(pe, step)


class Tile:

    def __init__(self, n, u, it, unroll, total):
        self.n, self.u, self.it, self.unroll, self.total = n, u, it, unroll, total

    def shift(self, k):
        v = self.u + k
        return Tile(self.n + k, v % self.unroll, self.it + v // self.unroll, self.unroll, self.total)

    @property
    def real(self):
        return not isinstance(self.n, int) or 0 <= self.n < self.total

    def at_least(self, k):
        return not isinstance(self.n, int) or self.n >= k


def pipelined(eng, total, unroll, before, after, step, peel=1):
    head = range(-before, peel * unroll)
    tail = range(total - unroll, total + after)
    for n in head:
        step(Tile(n, n % unroll, n // unroll, unroll, total))
    with eng.Fori(peel, total // unroll - 1) as it:
        for u in range(unroll):
            step(Tile(unroll * it + u, u, it, unroll, total))
    for n in tail:
        step(Tile(n, n % unroll, n // unroll, unroll, total))


def mix_phase(nc, ctx_rows, x, w_o, w_ra, b_r, iota8, x1_rows, xnT_cols, zm_cols, w_rows, w_sum):
    N, C = x.shape
    NT, CT = N // P, C // P
    E, R = 8, 8
    ER = E * R
    RW = ER + E
    BT = 4
    ZF0, WF0 = 2, 1
    LINKS = 19

    with Space(nc, "c_") as s:
        identity = s.sb("identity", [P, P])
        w_raw = s.sb("w_raw", [P, CT, C])
        w = s.sb("w", [P, 2, CT, C], F32R)
        wr_raw = s.sb("wr_raw", [P, CT, RW])
        wr = s.sb("wr", [P, 2, CT, RW], F32R)
        br_sb = s.sb("br_sb", [P, E])
        iota_sb = s.sb("iota_sb", [P, E])
        norm_consts = s.sb("norm_consts", [P, 3])
        ctx_in = s.sb("ctx_in", [P, 2, C])
        x_in = s.sb("x_in", [P, 2, C])
        cT = s.sb("cT", [P, 2, 2, CT, P], F32R)
        attn = s.sb("attn", [P, 2, C])
        x1 = s.sb("x1", [P, 2, C])
        xn = s.sb("xn", [P, 2, C])
        xnT = s.sb("xnT", [P, 2, 2, CT, P], F32R)
        stats = s.sb("stats", [P, 2, 2, 6])
        mean_var = s.sb("mean_var", [P, 2, 2, 2])
        coef = s.sb("coef", [P, 2, 2, 4])
        u1 = s.sb("u1", [P, BT, ER])
        small = {k: s.sb(k, [P, BT, E]) for k in ("logits", "centred", "expd", "probs", "equal", "cand", "hot1", "rest", "hot2", "twice1", "twice2", "delta")}
        one = {k: s.sb(k, [P, BT]) for k in ("top", "total", "recip", "w1", "first1", "w2", "first2")}
        z = s.sb("z", [P, 2, BT, ER])
        zs = s.sb("zs", [P, 2, BT, P], F32R)
        masks = s.sb("masks", [P, 2, BT, P])
        w_cols = s.sb("w_cols", [P, BT, P])
        zT = s.sb("zT", [P, 2, 4, P])
        wT = s.sb("wT", [2, BT * P])
        ps_cT = s.ps("ps_cT", [P, CT, P])
        ps_o = s.ps("ps_o", [P, 2, C])
        ps_xT = s.ps("ps_xT", [P, CT, P])
        ps_r = s.ps("ps_r", [P, 512])
        ps_z = s.ps("ps_z", [P, 2, 4, P])
        ps_w = s.ps("ps_w", [P, 512])
        rr = ps_r[:, 0:BT * RW].rearrange("p (t r) -> p t r", r=RW)

        id_made, norm_consts_made, cols_zeroed = s.sem("id_made"), s.sem("norm_consts_made"), s.sem("cols_zeroed")
        w_loaded, consts_loaded = s.sem("w_loaded"), s.sem("consts_loaded")
        w_hi, w_lo = s.sem("w_hi"), s.sem("w_lo")
        ctx_loaded, x_loaded = s.sems("ctx_loaded", 2), s.sems("x_loaded", 2)
        cT_in_psum, cT_hi, cT_lo = s.sem("cT_in_psum"), s.sem("cT_hi"), s.sem("cT_lo")
        o_done = s.sem("o_done")
        bn, stats_ready, eps_added, rstd_ready, shift_ready = (s.sems(k, 2) for k in ("bn", "stats", "eps", "rstd_r", "shift_r"))
        attn_ready, x1_ready, xn_ready = s.sem("attn_ready"), s.sem("x1_ready"), s.sem("xn_ready")
        x1_stored, xnT_stored = s.sems("x1_stored", 2), s.sems("xnT_stored", 2)
        xT_in_psum, xT_hi, xT_lo = s.sem("xT_in_psum"), s.sem("xT_hi"), s.sem("xT_lo")
        r_done = s.sem("r_done")
        chain = s.sem("chain")
        centred_ready, exp_ready = s.sem("centred_ready"), s.sem("exp_ready")
        hots_ready, masks_ready, z_ready = s.sem("hots_ready"), s.sem("masks_ready"), s.sem("z_ready")
        z_in_psum, z_out, w_in_psum, w_out = (s.sem(k) for k in ("z_in_psum", "z_out", "w_in_psum", "w_out"))
        z_stored, wT_stored = s.sems("z_stored", 2), s.sem("wT_stored")
        waited = s.sem("waited")
        block = s.block()
        STAGES = dict(total=NT, unroll=BT, before=3, after=2 * BT - 1, peel=2)

        def batch_of(t, back=1):
            b = t.it - back
            ok = not isinstance(b, int) or 0 <= b < NT // BT
            return b if ok else None

        @block.sync
        def _(sp):
            for u in range(2):
                sp.sem_inc(z_stored[u], 16)
            sp.sem_inc(wT_stored, 16)
            sp.dma_start(w_raw[:], w_o.rearrange("(c p) o -> p c o", p=P)).then_inc(w_loaded, 16)
            sp.dma_start(wr_raw[:], w_ra.rearrange("(c p) o -> p c o", p=P)).then_inc(w_loaded, 16)
            sp.dma_start(br_sb[:], b_r.partition_broadcast(P)).then_inc(consts_loaded, 16)
            sp.dma_start(iota_sb[:], iota8.partition_broadcast(P)).then_inc(consts_loaded, 16)

            def step(t):
                a = t.shift(3)
                if a.real:
                    if a.at_least(2):
                        sp.wait_ge(cT_in_psum, a.n - 1)
                    sp.dma_start(ctx_in[:, a.u % 2], ctx_rows[bass.ds(a.n * P, P), :]).then_inc(ctx_loaded[a.u % 2], 16)
                d = t.shift(2)
                if d.real:
                    if d.at_least(2):
                        sp.wait_ge(x1_ready, d.n - 1)
                    sp.dma_start(x_in[:, d.u % 2], x[bass.ds(d.n * P, P), :]).then_inc(x_loaded[d.u % 2], 16)
                if t.real:
                    wait_apart(sp, x1_ready, t.n + 1, waited)
                    sp.dma_start(x1_rows[bass.ds(t.n * P, P), :], x1[:, t.u % 2]).then_inc(x1_stored[t.u % 2], 16)
                c = t.shift(-1)
                if c.real:
                    wait_apart(sp, xT_lo, c.n + 1, waited)
                    for a_ in range(2):
                        sp.dma_start(xnT_cols[:, a_, :, bass.ds(c.n * P, P)], xnT[:, c.u % 2, a_].bitcast(F32)).then_inc(xnT_stored[c.u % 2], 16)
                b = batch_of(t, 2)
                if b is not None and t.u == 1:
                    sp.wait_ge(w_out, WF0 + b + 1)
                    sp.dma_start(w_rows[:, bass.ds(b * BT * P, BT * P)], wT[:]).then_inc(wT_stored, 16)
                if b is not None and t.u in (1, 2):
                    for k in (2 * t.u - 2, 2 * t.u - 1):
                        m = b * BT + k
                        sp.wait_ge(z_out, ZF0 + m + 1)
                        sp.dma_start(zm_cols[:, :, bass.ds(m * P, P)], zT[:, k % 2]).then_inc(z_stored[k % 2], 16)

            pipelined(sp, step=step, **STAGES)
            for u in range(2):
                sp.wait_ge(x1_stored[u], 16 * (NT // 2))
                sp.wait_ge(xnT_stored[u], 32 * (NT // 2))
                sp.wait_ge(z_stored[u], 16 * (NT // 2 + 1))
            sp.wait_ge(wT_stored, 16 * (NT // BT + 1))

        def slot_uses(t, per=16):
            return per * (2 * t.it + t.u // 2)

        @block.gpsimd
        def _(pool):
            make_identity(nc, pool, identity, id_made)
            nc.gpsimd.memset(w_cols[:], 0.0).then_inc(cols_zeroed, 1)
            make_norm_constants(nc, pool, norm_consts, norm_consts_made)

            def coefficients(j, t):
                layer_norm_coefficients(nc, pool, norm_consts, mean_var[:, j, t.u % 2], coef[:, j, t.u % 2],
                                        stats_ready[j], eps_added[j], rstd_ready[j], shift_ready[j], t.n + 1)

            def step(t):
                if t.real:
                    coefficients(1, t)
                d = t.shift(1)
                if d.real:
                    coefficients(0, d)

            pipelined(pool, step=step, **STAGES)

        @block.scalar
        def _(act):
            act.sem_inc(z_out, ZF0)
            act.sem_inc(w_out, WF0)
            act.wait_ge(w_loaded, 32)
            nc.scalar.activation(w[:, 0], w_raw[:], ACT.Copy)
            nc.scalar.activation(wr[:, 0], wr_raw[:], ACT.Copy).then_inc(w_hi, 1)

            def step(t):
                c = t.shift(-1)
                if c.real:
                    act.wait_ge(xT_in_psum, c.n + 1)
                    if c.at_least(2):
                        act.wait_ge(r_done, c.n - 1)
                        act.wait_ge(xnT_stored[c.u % 2], slot_uses(c, 32))
                    nc.scalar.activation(xnT[:, c.u % 2, 0], ps_xT[:], ACT.Copy).then_inc(xT_hi, 1)
                a = t.shift(2)
                if a.real:
                    act.wait_ge(cT_in_psum, a.n + 1)
                    if a.at_least(2):
                        act.wait_ge(o_done, a.n - 1)
                    nc.scalar.activation(cT[:, a.u % 2, 0], ps_cT[:], ACT.Copy).then_inc(cT_hi, 1)
                if t.real:
                    u = t.u % 2
                    act.wait_ge(shift_ready[1], t.n + 1)
                    if t.at_least(2):
                        act.wait_ge(xT_in_psum, t.n - 1)
                    nc.scalar.activation(xn[:, u], x1[:, u], ACT.Identity, bias=coef[:, 1, u, 3:4],
                                         scale=coef[:, 1, u, 2:3]).then_inc(xn_ready, 1)
                b = batch_of(t)
                if b is not None and t.u == 2:
                    act.wait_ge(centred_ready, b + 1)
                    nc.scalar.activation(small["expd"][:], small["centred"][:], ACT.Exp).then_inc(exp_ready, 1)
                d = t.shift(1)
                if d.real:
                    u = d.u % 2
                    act.wait_ge(shift_ready[0], d.n + 1)
                    if d.at_least(2):
                        act.wait_ge(x1_ready, d.n - 1)
                    nc.scalar.activation(attn[:, u], ps_o[:, u], ACT.Identity, bias=coef[:, 0, u, 3:4],
                                         scale=coef[:, 0, u, 2:3]).then_inc(attn_ready, 1)
                b = batch_of(t, 2)
                if b is not None and t.u == 1:
                    act.wait_ge(w_in_psum, b + 1)
                    act.wait_ge(wT_stored, 16 * (b + 1))
                    nc.scalar.activation(wT[:], ps_w[0:2, :], ACT.Copy).then_inc(w_out, 1)
                if b is not None and t.u in (1, 2):
                    for k in (2 * t.u - 2, 2 * t.u - 1):
                        m = b * BT + k
                        act.wait_ge(z_in_psum, m + 1)
                        act.wait_ge(z_stored[k % 2], 16 * (2 * b + k // 2 + 1))
                        nc.scalar.activation(zT[:, k % 2], ps_z[:, k % 2], ACT.Copy).then_inc(z_out, 1)

            pipelined(act, step=step, **STAGES)

        @block.vector
        def _(dve):
            dve.wait_ge(w_hi, 1)
            nc.vector.tensor_tensor(w[:, 1], w_raw[:], w[:, 0].bitcast(F32), ALU.subtract)
            nc.vector.tensor_tensor(wr[:, 1], wr_raw[:], wr[:, 0].bitcast(F32), ALU.subtract).then_inc(w_lo, 1)
            dve.wait_ge(consts_loaded, 32)
            dve.wait_ge(cols_zeroed, 1)

            def statistics(j, t, src):
                u = t.u % 2
                nc.vector.bn_stats(stats[:, j, u], src).then_inc(bn[j], 1)
                wait_apart(dve, bn[j], t.n + 1, waited)
                nc.vector.bn_aggr(mean_var[:, j, u], stats[:, j, u]).then_inc(stats_ready[j], 1)


            def route(b, part):
                links = [(0, 2, 11)[part]]

                def link(ins):
                    links[0] += 1
                    ins.then_inc(chain, 1)
                    dve.wait_ge(chain, LINKS * b + links[0])

                V, S, O = nc.vector, small, one

                def wide(v):
                    return v[:].unsqueeze(2).broadcast_to([P, BT, E])

                iota = iota_sb[:].unsqueeze(1).broadcast_to([P, BT, E])
                if part == 0:
                    dve.wait_ge(r_done, BT * (b + 1))
                    V.tensor_copy(u1[:], rr[:, :, 0:ER])
                    link(V.tensor_tensor(S["logits"][:], rr[:, :, ER:RW], br_sb[:].unsqueeze(1).broadcast_to([P, BT, E]), ALU.add))
                    link(V.tensor_reduce(O["top"][:], S["logits"][:], AX_X, ALU.max))
                    V.tensor_tensor(S["centred"][:], S["logits"][:], wide(O["top"]), ALU.subtract).then_inc(centred_ready, 1)
                    return
                if part == 1:
                    dve.wait_ge(exp_ready, b + 1)
                    link(V.tensor_reduce(O["total"][:], S["expd"][:], AX_X, ALU.add))
                    link(V.reciprocal(O["recip"][:], O["total"][:]))
                    link(V.tensor_tensor(S["probs"][:], S["expd"][:], wide(O["recip"]), ALU.mult))
                src, wt, first, hot = (("probs", "w1", "first1", "hot1"), ("rest", "w2", "first2", "hot2"))[part - 1]
                link(V.tensor_reduce(O[wt][:], S[src][:], AX_X, ALU.max))
                link(V.tensor_tensor(S["equal"][:], S[src][:], wide(O[wt]), ALU.is_equal))
                link(V.tensor_tensor(S["cand"][:], S["equal"][:], iota, ALU.mult))
                link(V.tensor_reduce(O[first][:], S["cand"][:], AX_X, ALU.min))
                link(V.tensor_tensor(S[hot][:], iota, wide(O[first]), ALU.is_equal))
                if part == 1:
                    link(V.scalar_tensor_tensor(S["rest"][:], S["hot1"][:], -2.0, S["probs"][:], ALU.mult, ALU.add))
                    return
                dve.wait_ge(z_out, ZF0 + BT * b)
                dve.wait_ge(w_out, WF0 + b)
                V.tensor_scalar(S["twice1"][:], S["hot1"][:], 2.0, None, ALU.mult)
                link(V.tensor_scalar(S["twice2"][:], S["hot2"][:], 2.0, None, ALU.mult))
                V.tensor_copy(w_cols[:, :, 0], O["w1"][:])
                V.tensor_copy(w_cols[:, :, 1], O["w2"][:])
                V.tensor_tensor(w_sum[:, bass.ds(b * BT, BT)], O["w1"][:], O["w2"][:], ALU.add)
                V.tensor_tensor(S["delta"][:], S["twice2"][:], S["twice1"][:], ALU.subtract).then_inc(hots_ready, 1)
                dve.wait_ge(hots_ready, b + 1)
                for k, name in enumerate(("twice1", "twice2")):
                    src = small[name][:].unsqueeze(3).broadcast_to([P, BT, E, R])
                    for c in range(2):
                        last = V.tensor_copy(masks[:, k, :, c * ER:(c + 1) * ER].rearrange("p t (e r) -> p t e r", r=R), src)
                last.then_inc(masks_ready, 1)
                for k, name in enumerate(("twice1", "delta")):
                    last = V.tensor_tensor(z[:, k].rearrange("p t (e r) -> p (t e) r", r=R), u1[:].rearrange("p t (e r) -> p (t e) r", r=R),
                                           S[name][:].rearrange("p t e -> p (t e)").unsqueeze(2).broadcast_to([P, BT * E, R]), ALU.mult)
                link(last)
                link(V.tensor_copy(zs[:, :, :, 0:ER], z[:]))
                V.tensor_tensor(zs[:, :, :, ER:2 * ER], z[:], zs[:, :, :, 0:ER].bitcast(F32), ALU.subtract).then_inc(z_ready, 1)
                assert links[0] == LINKS, links

            def step(t):
                if t.real:
                    dve.wait_ge(x1_ready, t.n + 1)
                    statistics(1, t, x1[:, t.u % 2])
                c = t.shift(-1)
                if c.real:
                    dve.wait_ge(xT_hi, c.n + 1)
                    nc.vector.tensor_tensor(xnT[:, c.u % 2, 1], ps_xT[:], xnT[:, c.u % 2, 0].bitcast(F32), ALU.subtract).then_inc(xT_lo, 1)
                a = t.shift(2)
                if a.real:
                    dve.wait_ge(cT_hi, a.n + 1)
                    nc.vector.tensor_tensor(cT[:, a.u % 2, 1], ps_cT[:], cT[:, a.u % 2, 0].bitcast(F32), ALU.subtract).then_inc(cT_lo, 1)
                b = batch_of(t, 2 if t.u == 0 else 1)
                if b is not None and t.u != 1:
                    route(b, (t.u + 2) % BT)
                d = t.shift(1)
                if d.real:
                    dve.wait_ge(o_done, d.n + 1)
                    statistics(0, d, ps_o[:, d.u % 2])
                    u = d.u % 2
                    dve.wait_ge(attn_ready, d.n + 1)
                    if d.at_least(2):
                        dve.wait_ge(x1_stored[u], slot_uses(d))
                        dve.wait_ge(xn_ready, d.n - 1)
                    dve.wait_ge(x_loaded[u], slot_uses(d) + 16)
                    nc.vector.tensor_tensor(x1[:, u], x_in[:, u], attn[:, u], ALU.add).then_inc(x1_ready, 1)

            pipelined(dve, step=step, **STAGES)

        @block.tensor
        def _(pe):
            pe.wait_ge(id_made, 2)

            def step(t):
                c = t.shift(-1)
                if c.real:
                    pe.wait_ge(xn_ready, c.n + 1)
                    if c.at_least(1):
                        pe.wait_ge(xT_lo, c.n)
                    for k in range(CT):
                        last = nc.tensor.transpose(ps_xT[:, k], xn[:, c.u % 2, k * P:(k + 1) * P], identity[:])
                    last.then_inc(xT_in_psum, 1)
                a = t.shift(2)
                if a.real:
                    u = a.u % 2
                    pe.wait_ge(ctx_loaded[u], slot_uses(a) + 16)
                    if a.at_least(1):
                        pe.wait_ge(cT_lo, a.n)
                    for k in range(CT):
                        last = nc.tensor.transpose(ps_cT[:, k], ctx_in[:, u, k * P:(k + 1) * P], identity[:])
                    last.then_inc(cT_in_psum, 1)
                d = t.shift(1)
                if d.real:
                    u = d.u % 2
                    if isinstance(d.n, int) and d.n == 0:
                        pe.wait_ge(w_lo, 1)
                    pe.wait_ge(cT_lo, d.n + 1)
                    if d.at_least(2):
                        pe.wait_ge(attn_ready, d.n - 1)
                    k = 0
                    for q in range(CT):
                        for x_, w_ in SPLIT_PAIRS:
                            last = nc.tensor.matmul(ps_o[:, u], cT[:, u, x_, q], w[:, w_, q], start=k == 0, stop=k == 3 * CT - 1)
                            k += 1
                    last.then_inc(o_done, 1)
                c = t.shift(-2)
                if c.real:
                    u = c.u % 2
                    pe.wait_ge(xT_lo, c.n + 1)
                    if c.u == 0 and c.at_least(1):
                        pe.wait_ge(chain, LINKS * (c.it - 1) + 1)
                    k = 0
                    for q in range(CT):
                        for x_, w_ in SPLIT_PAIRS:
                            last = nc.tensor.matmul(rr[:, c.u], xnT[:, u, x_, q], wr[:, w_, q], start=k == 0, stop=k == 3 * CT - 1)
                            k += 1
                    last.then_inc(r_done, 1)
                b = batch_of(t, 2)
                if b is not None and t.u in (1, 2):
                    if t.u == 1:
                        pe.wait_ge(z_ready, b + 1)
                        pe.wait_ge(masks_ready, b + 1)
                        pe.wait_ge(w_out, WF0 + b)
                        for k in range(BT):
                            last = nc.tensor.transpose(ps_w[:, k * P:(k + 1) * P], w_cols[:, k], identity[:])
                        last.then_inc(w_in_psum, 1)
                    for k in (2 * t.u - 2, 2 * t.u - 1):
                        pe.wait_ge(z_out, ZF0 + b * BT + k - 1)
                        srcs = [zs[:, 0, k].bitcast(F32), zs[:, 1, k].bitcast(F32), masks[:, 0, k], masks[:, 1, k]]
                        for q, src in enumerate(srcs):
                            last = nc.tensor.transpose(ps_z[:, k % 2, q], src, identity[:])
                        last.then_inc(z_in_psum, 1)

            pipelined(pe, step=step, **STAGES)


class ExpertWeights:

    def __init__(self, s, C, F, ER):
        CT, FT = C // P, F // P
        self.w1 = s.sb("w1", [P, 2, CT, F], F32R)
        self.w2 = s.sb("w2", [P, 2, FT, C], F32R)
        self.a2 = s.sb("a2", [P, FT, 2 * ER], F32R)
        self.b1 = s.sb("b1", [P, F], F32R)
        self.ER = ER
        self.b2 = s.sb("b2", [P, 2, C], F32R)


def load_experts(nc, wts, w1, w2, a2, b1, b2):
    C, F = w1.shape
    ER = a2.shape[1]
    CT, FT = C // P, F // P
    with Space(nc, "d_") as s:
        BUFS = 4
        raw = s.sb("raw", [P, BUFS, 2048])
        loaded = s.sems("loaded", BUFS)
        hi_ready, lo_ready = s.sem("hi_ready"), s.sem("lo_ready")
        jobs = []
        w1v, w2v = w1.rearrange("(c p) f -> p c f", p=P), w2.rearrange("(t p) o -> p t o", p=P)
        for c in range(CT):
            jobs.append(([(slice(0, P), w1v[:, c])], wts.w1[:, 0, c], wts.w1[:, 1, c], lambda r: r))
        for t in range(0, FT, 4):
            jobs.append(([(slice(0, P), w2v[:, t:t + 4])], wts.w2[:, 0, t:t + 4], wts.w2[:, 1, t:t + 4],
                         lambda r: r.rearrange("p (t o) -> p t o", t=4)))
        jobs.append(([(slice(0, P), a2.rearrange("(t p) e -> p t e", p=P))], wts.a2[:, :, 0:ER], wts.a2[:, :, ER:2 * ER],
                     lambda r: r[:, 0:FT * ER].rearrange("p (t e) -> p t e", t=FT)))
        jobs.append(([(slice(0, ER), b1), (slice(ER, 2 * ER), b1)], wts.b1[:], wts.b1[ER:2 * ER], lambda r: r))
        jobs.append(([(slice(0, ER), b2), (slice(ER, 2 * ER), b2)], wts.b2[:, 0], wts.b2[:, 1], lambda r: r[:, 0:C]))
        landed, count = [], [0] * BUFS
        for k, (dmas, *_) in enumerate(jobs):
            count[k % BUFS] += 16 * len(dmas)
            landed.append(count[k % BUFS])
        block = s.block()

        @block.sync
        def _(sp):
            for k, (dmas, hi, lo, view) in enumerate(jobs):
                if k >= BUFS:
                    sp.wait_ge(lo_ready, k - BUFS + 1)
                for rows, src in dmas:
                    sp.dma_start(view(raw[:, k % BUFS])[rows], src).then_inc(loaded[k % BUFS], 16)

        @block.scalar
        def _(act):
            for k, (dmas, hi, lo, view) in enumerate(jobs):
                act.wait_ge(loaded[k % BUFS], landed[k])
                nc.scalar.activation(hi, view(raw[:, k % BUFS]), ACT.Copy).then_inc(hi_ready, 1)

        @block.vector
        def _(dve):
            for k, (dmas, hi, lo, view) in enumerate(jobs):
                rows = slice(P - lo.shape[0], P)
                dve.wait_ge(hi_ready, k + 1)
                nc.vector.tensor_tensor(lo, view(raw[:, k % BUFS])[rows], hi[rows].bitcast(F32), ALU.subtract).then_inc(lo_ready, 1)


def expert_phase(nc, wts, xnT_cols, zm_cols, w_rows, w_sum, x1_rows, b1_cols, b2_row, out):
    N, C = out.shape
    CT, FT = C // P, wts.w2.shape[2]
    G = 256
    NG, GT = N // G, G // P
    ER = wts.ER
    RH = 2

    with Space(nc, "e_") as s:
        b1_sb = s.sb("b1_sb", [P, FT])
        b2_sb = s.sb("b2_sb", [P, C])
        norm_consts = s.sb("norm_consts", [P, 3])
        xT = s.sb("xT", [P, 2, 2, CT, G], F32R)
        z_hi = s.sb("z_hi", [P, 2, 2, G], F32R)
        z_lo = s.sb("z_lo", [ER, 2, 2, G], F32R)
        masks = s.sb("masks", [P, 2, G])
        wk = s.sb("wk", [P, 2, 2, G])
        h = s.sb("h", [P, 2, 3, G])
        h_hi = s.sb("h_hi", [P, 2, 3, G], F32R)
        h_lo = s.sb("h_lo", [P, 2, 3, G], F32R)
        z2 = s.sb("z2", [P, 2, G])
        z2s = s.sb("z2s", [P, 2, G], F32R)
        y = s.sb("y", [P, C])
        x1_in = s.sb("x1_in", [P, C])
        stats = s.sb("stats", [P, 6])
        mean_var = s.sb("mean_var", [P, 2])
        coef = s.sb("coef", [P, 4])
        ps_h = s.ps("ps_h", [P, RH, 512])
        ps_u = s.ps("ps_u", [P, 2, G])
        ps_y = s.ps("ps_y", [P, 2, GT, C])

        norm_consts_made = s.sem("norm_consts_made")
        consts_loaded = s.sem("consts_loaded")
        x_loaded, z_loaded, wk_loaded = s.sems("x_loaded", 2), s.sems("z_loaded", 2), s.sems("wk_loaded", 2)
        masks_loaded = s.sem("masks_loaded")
        x1_loaded = s.sem("x1_loaded")
        base_done, moved_done = s.sem("base_done"), s.sem("moved_done")
        h0_ready, h1_ready = s.sem("h0_ready"), s.sem("h1_ready")
        g_ready, hi_ready, lo_ready = s.sem("g_ready"), s.sem("hi_ready"), s.sem("lo_ready")
        used = s.sem("used")
        masked, z2_sum, z2_hi, z2_ready = s.sem("masked"), s.sem("z2_sum"), s.sem("z2_hi"), s.sem("z2_ready")
        y_done, y_ready = s.sem("y_done"), s.sem("y_ready")
        bn, stats_ready, eps_added, rstd_ready, shift_ready = (s.sem(k) for k in ("bn", "stats_r", "eps", "rstd_r", "shift_r"))
        y_normed, out_ready = s.sem("y_normed"), s.sem("out_ready")
        out_stored = s.sem("out_stored")
        waited = s.sem("waited")
        block = s.block()

        STAGES = dict(total=NG, unroll=2, before=0, after=1)

        def bank(t, f):
            return f % 2

        def F(t, f):
            return FT * t.n + f

        @block.sync
        def _(sp):
            sp.dma_start(b1_sb[:], b1_cols).then_inc(consts_loaded, 16)
            sp.dma_start(b2_sb[:], b2_row.partition_broadcast(P)).then_inc(consts_loaded, 16)

            def load(t):
                u, cols = t.u, bass.ds(t.n * G, G)
                for a in range(2):
                    sp.dma_start(xT[:, u, a].bitcast(F32), xnT_cols[:, a, :, cols]).then_inc(x_loaded[u], 16)
                for dst, src in ((z_hi[0:ER, u], 0), (z_hi[ER:2 * ER, u], 0), (z_lo[:, u], ER)):
                    sp.dma_start(dst.bitcast(F32), zm_cols[src:src + ER, 0:2, cols]).then_inc(z_loaded[u], 16)
                for k in range(2):
                    sp.dma_start(wk[:, u, k], w_rows[k, cols].partition_broadcast(P)).then_inc(wk_loaded[u], 16)

            def step(t):
                if isinstance(t.n, int) and t.n == 0:
                    load(t)
                n = t.shift(1)
                if n.real and t.real:
                    if n.at_least(2):
                        sp.wait_ge(used, F(t, 0))
                    load(n)
                if t.real:
                    if t.at_least(1):
                        sp.wait_ge(masked, t.n)
                    sp.dma_start(masks[:], zm_cols[:, 2:4, bass.ds(t.n * G, G)]).then_inc(masks_loaded, 16)
                p = t.shift(-1)
                if p.real:
                    for j in range(GT):
                        m = GT * p.n + j
                        if not (isinstance(p.n, int) and p.n == 0 and j == 0):
                            sp.wait_ge(out_stored, 16 * m)
                        rows = bass.ds((GT * p.n + j) * P, P)
                        sp.dma_start(x1_in[:], x1_rows[rows, :]).then_inc(x1_loaded, 16)
                        sp.wait_ge(out_ready, m + 1)
                        sp.dma_start(out[rows, :], x1_in[:]).then_inc(out_stored, 16)

            pipelined(sp, step=step, **STAGES)
            sp.wait_ge(out_stored, 16 * NG * GT)

        @block.gpsimd
        def _(pool):
            make_norm_constants(nc, pool, norm_consts, norm_consts_made)

            def step(t):
                p = t.shift(-1)
                if p.real:
                    for j in range(GT):
                        m = GT * p.n + j
                        layer_norm_coefficients(nc, pool, norm_consts, mean_var, coef,
                                                stats_ready, eps_added, rstd_ready, shift_ready, m + 1)
                        pool.wait_ge(y_normed, m + 1)
                        pool.wait_ge(x1_loaded, 16 * (m + 1))
                        nc.gpsimd.tensor_tensor(x1_in[:], x1_in[:], y[:], ALU.add).then_inc(out_ready, 1)

            pipelined(pool, step=step, **STAGES)

        @block.scalar
        def _(act):
            act.wait_ge(consts_loaded, 32)

            def gelu(t, f, k):
                n = F(t, f)
                act.wait_ge((base_done, moved_done)[k], n + 1)
                if not (isinstance(n, int) and n < 2):
                    act.wait_ge(lo_ready, 3 * (n - 1))
                nc.scalar.activation(h[:, f % 2, k], ps_h[:, bank(t, f), 0:G], ACT.Gelu_apprx_tanh,
                                     bias=b1_sb[:, f:f + 1]).then_inc((h0_ready, h1_ready)[k], 1)

            def step(t):
                p = t.shift(-1)
                for f in range(FT):
                    if t.real:
                        gelu(t, f, 0)
                        gelu(t, f, 1)
                    if p.real and f in (4, 8):
                        m = GT * p.n + (f == 8)
                        act.wait_ge(shift_ready, m + 1)
                        nc.scalar.activation(y[:], y[:], ACT.Identity, bias=coef[:, 3:4], scale=coef[:, 2:3]).then_inc(y_normed, 1)

            pipelined(act, step=step, **STAGES)

        @block.vector
        def _(dve):
            def scale(t, f):
                n, b = F(t, f), f % 2
                V = nc.vector
                if f == 0:
                    dve.wait_ge(wk_loaded[t.u], 32 * (t.it + 1))
                dve.wait_ge(h0_ready, n + 1)
                V.tensor_tensor(h[:, b, 0], h[:, b, 0], wk[:, t.u, 0], ALU.mult).then_inc(g_ready, 1)
                if not (isinstance(n, int) and n < 2):
                    dve.wait_ge(used, n - 1)
                dve.wait_ge(g_ready, 3 * n + 1)
                V.tensor_copy(h_hi[:, b, 0], h[:, b, 0]).then_inc(hi_ready, 1)
                dve.wait_ge(hi_ready, 2 * n + 1)
                V.tensor_tensor(h_lo[:, b, 0], h[:, b, 0], h_hi[:, b, 0].bitcast(F32), ALU.subtract).then_inc(lo_ready, 1)
                dve.wait_ge(h1_ready, n + 1)
                V.tensor_tensor(h[:, b, 1], h[:, b, 1], wk[:, t.u, 1], ALU.mult).then_inc(g_ready, 1)
                dve.wait_ge(g_ready, 3 * n + 2)
                V.tensor_tensor(h[:, b, 2], h[:, b, 0], h[:, b, 1], ALU.add).then_inc(g_ready, 1)
                dve.wait_ge(g_ready, 3 * n + 3)
                V.tensor_copy(h_hi[:, b, 1:3], h[:, b, 1:3]).then_inc(hi_ready, 1)
                dve.wait_ge(hi_ready, 2 * n + 2)
                V.tensor_tensor(h_lo[:, b, 1:3], h[:, b, 1:3], h_hi[:, b, 1:3].bitcast(F32), ALU.subtract).then_inc(lo_ready, 2)

            def mask(p):
                V = nc.vector
                dve.wait_ge(used, F(p, FT))
                dve.wait_ge(masks_loaded, 16 * (p.n + 1))
                for k in range(2):
                    last = V.tensor_tensor(z2[:, k], ps_u[:, k], masks[:, k], ALU.mult)
                last.then_inc(masked, 1)
                dve.wait_ge(masked, p.n + 1)
                V.tensor_tensor(z2[:, 0], z2[:, 0], z2[:, 1], ALU.add).then_inc(z2_sum, 1)
                dve.wait_ge(z2_sum, p.n + 1)
                if p.at_least(1):
                    dve.wait_ge(y_done, GT * p.n)
                V.tensor_copy(z2s[:, 0], z2[:, 0]).then_inc(z2_hi, 1)
                dve.wait_ge(z2_hi, p.n + 1)
                V.tensor_tensor(z2s[:, 1], z2[:, 0], z2s[:, 0].bitcast(F32), ALU.subtract).then_inc(z2_ready, 1)

            def close(p, j):
                m = GT * p.n + j
                V = nc.vector
                dve.wait_ge(y_done, m + 1)
                if not (isinstance(m, int) and m == 0):
                    dve.wait_ge(out_ready, m)
                V.scalar_tensor_tensor(y[:], b2_sb[:], w_sum[:, bass.ds(m, 1)], ps_y[:, p.u, j], ALU.mult, ALU.add).then_inc(y_ready, 1)
                dve.wait_ge(y_ready, m + 1)
                V.bn_stats(stats[:], y[:]).then_inc(bn, 1)
                wait_apart(dve, bn, m + 1, waited)
                V.bn_aggr(mean_var[:], stats[:]).then_inc(stats_ready, 1)

            def step(t):
                p = t.shift(-1)
                for f in range(FT):
                    if t.real:
                        scale(t, f)
                    if p.real and f == 0:
                        mask(p)
                    if p.real and f in (3, 7):
                        close(p, int(f == 7))

            dve.wait_ge(consts_loaded, 32)
            pipelined(dve, step=step, **STAGES)

        @block.tensor
        def _(pe):
            def base(t, f):
                u, n, b = t.u, F(t, f), bank(t, f)
                if f == 0:
                    pe.wait_ge(x_loaded[u], 32 * (t.it + 1))
                    pe.wait_ge(z_loaded[u], 48 * (t.it + 1))
                if not (isinstance(n, int) and n < 2):
                    pe.wait_ge(h1_ready, n - 1)
                cols = slice(f * P, (f + 1) * P)
                first = True
                for c in range(CT):
                    for x_, w_ in SPLIT_PAIRS:
                        nc.tensor.matmul(ps_h[:, b, 0:G], wts.w1[:, w_, c, cols], xT[:, u, x_, c], start=first, stop=False,
                                         skip_group_check=True)
                        first = False
                low_rank(t, f, 0).then_inc(base_done, 1)

            def low_rank(t, f, k):
                cols = slice(f * P, (f + 1) * P)
                dst = ps_h[:, bank(t, f), 0:G]
                nc.tensor.matmul(dst, wts.b1[0:ER, cols], z_lo[:, t.u, k], start=False, stop=False, skip_group_check=True)
                return nc.tensor.matmul(dst, wts.b1[:, cols], z_hi[:, t.u, k], start=False, stop=False, skip_group_check=True)

            def moved(t, f):
                pe.wait_ge(h0_ready, F(t, f) + 1)
                low_rank(t, f, 1).then_inc(moved_done, 1)

            def down(t, f):
                n, b = F(t, f), f % 2
                pe.wait_ge(lo_ready, 3 * n + 3)
                if f == 0 and t.at_least(1):
                    pe.wait_ge(masked, t.n)
                for k in range(2):
                    for q, part in enumerate((h_hi, h_lo)):
                        nc.tensor.matmul(ps_u[:, k], wts.a2[:, f], part[:, b, k], start=f == 0 and k == 0 and q == 0, stop=False,
                                         skip_group_check=True)
                if f == 0 and t.at_least(2):
                    pe.wait_ge(y_ready, GT * (t.n - 1))
                for j in range(GT):
                    rows = slice(j * P, (j + 1) * P)
                    for q, (x_, w_) in enumerate(SPLIT_PAIRS):
                        last = nc.tensor.matmul(ps_y[:, t.u, j], (h_hi, h_lo)[x_][:, b, 2, rows], wts.w2[:, w_, f],
                                                start=f == 0 and q == 0, stop=False, skip_group_check=True)
                last.then_inc(used, 1)

            def close(p):
                pe.wait_ge(z2_ready, p.n + 1)
                for j in range(GT):
                    rows = slice(j * P, (j + 1) * P)
                    for q, (x_, w_) in enumerate(SPLIT_PAIRS):
                        last = nc.tensor.matmul(ps_y[:, p.u, j], z2s[:, x_, rows], wts.b2[:, w_], start=False, stop=q == 2,
                                                skip_group_check=True)
                    last.then_inc(y_done, 1)

            def step(t):
                p = t.shift(-1)
                if isinstance(t.n, int) and t.n == 0:
                    base(t, 0)
                for f in range(FT):
                    if t.real:
                        if f + 1 < FT:
                            base(t, f + 1)
                        elif t.shift(1).real:
                            base(t.shift(1), 0)
                        moved(t, f)
                        if f > 0:
                            down(t, f - 1)
                        elif p.real:
                            down(p, FT - 1)
                    elif p.real and f == 0:
                        down(p, FT - 1)
                    if p.real and f == 2:
                        close(p)

            pipelined(pe, step=step, **STAGES)


def rope_table(T, D=32, base=10000.0):
    f32 = np.float32
    inv = (f32(1.0) / f32(base) ** (np.arange(0, D, 2, dtype=f32) / f32(D))).astype(f32)
    ang = np.outer(np.arange(T, dtype=f32), inv)
    cos, sin = np.cos(ang), np.sin(ang)
    return np.concatenate([cos, cos, -sin, sin], axis=1)


def mask_tables(T, block=64):
    before = np.zeros((32, T), np.float32)
    inside = np.zeros((32, T), np.float32)
    q = np.arange(T)
    for b in range(T // block):
        before[b] = q < block * b
        inside[b] = np.where(q // block == b, np.float32(-2.0**60), np.float32(0))
    inside[16:18] = 1.0
    return before, inside, np.ascontiguousarray(before[:16].T)


def build_program(nc, t, out):
    N, C = t["x"].shape
    F = t["w1"].shape[1]
    ER = t["a2"].shape[1]

    def scratch(name, *shape):
        return nc.dram_tensor(name, list(shape), F32, kind="Internal").ap()

    q_rows, k_rows, v_rows = (scratch(n, N, C) for n in ("q_rows", "k_rows", "v_rows"))
    ctx_rows, x1_rows = scratch("ctx_rows", N, C), scratch("x1_rows", N, C)
    xnT_cols = scratch("xnT_cols", P, 2, C // P, N)
    zm_cols = scratch("zm_cols", 2 * ER, 4, N)
    w_rows = scratch("w_rows", 2, N)

    project_phase(nc, t["x"], t["w_qkv"], t["rope"], q_rows, k_rows, v_rows)
    attention_phase(nc, q_rows, k_rows, v_rows, t["aux_q"], t["aux_k"], t["q_first_of_block"], ctx_rows)
    with Space(nc, "f_") as s:
        w_sum = s.sb("w_sum", [P, N // P])
        mix_phase(nc, ctx_rows, t["x"], t["w_o"], t["w_ra"], t["b_r"], t["iota8"],
                  x1_rows, xnT_cols, zm_cols, w_rows, w_sum)
        wts = ExpertWeights(s, C, F, ER)
        load_experts(nc, wts, t["w1"], t["w2"], t["a2"], t["b1_lora"], t["b2_lora"])
        expert_phase(nc, wts, xnT_cols, zm_cols, w_rows, w_sum, x1_rows, t["b1_cols"], t["b2"], out)


def kernel(L0_attn_x, L0_attn_w_q, L0_attn_w_k, L0_attn_w_v, L0_attn_w_o, L0_ffn_W_r, L0_ffn_b_r,
           L0_ffn_W1, L0_ffn_b1, L0_ffn_W2, L0_ffn_b2, L0_ffn_A1, L0_ffn_B1, L0_ffn_A2, L0_ffn_B2):
    import concourse.bacc as bacc
    from concourse.bass_utils import run_bass_kernel_spmd

    B, T, C = L0_attn_x.shape
    E, R, F = L0_ffn_A2.shape
    before, inside, q_first_of_block = mask_tables(T)
    inputs = {
        "x": L0_attn_x.reshape(B * T, C),
        "w_qkv": np.concatenate([L0_attn_w_q.T, L0_attn_w_k.T, L0_attn_w_v.T], axis=1),
        "rope": rope_table(T),
        "aux_q": before,
        "aux_k": inside,
        "q_first_of_block": q_first_of_block,
        "w_o": L0_attn_w_o.T,
        "w_ra": np.concatenate([L0_ffn_A1.reshape(E * R, C), L0_ffn_W_r], axis=0).T,
        "b_r": L0_ffn_b_r,
        "iota8": np.arange(-E, 0).astype(np.float32),
        "w1": L0_ffn_W1.T,
        "w2": L0_ffn_W2.T,
        "a2": L0_ffn_A2.reshape(E * R, F).T,
        "b1_lora": L0_ffn_B1.transpose(0, 2, 1).reshape(E * R, F),
        "b2_lora": L0_ffn_B2.transpose(0, 2, 1).reshape(E * R, C),
        "b1_cols": L0_ffn_b1.reshape(F // P, P).T,
        "b2": L0_ffn_b2,
    }
    inputs = {name: np.ascontiguousarray(a) for name, a in inputs.items()}
    nc = bacc.Bacc("TRN2", target_bir_lowering=False, num_devices=1)
    tensors = {name: nc.dram_tensor(name, list(a.shape), F32, kind="ExternalInput").ap() for name, a in inputs.items()}
    out = nc.dram_tensor("out", [B * T, C], F32, kind="ExternalOutput").ap()
    build_program(nc, tensors, out)
    result = run_bass_kernel_spmd(nc, [inputs], core_ids=[0])
    return result.results[0]["out"].reshape(B, T, C)
```
